# Optimizing a Trainium2 kernel written in Bass

```python
import numpy as np
import jax
import jax.numpy as jnp

def _softmax(x, axis=-1):
    return jax.nn.softmax(x, axis=axis)

def _gelu(x):
    return jax.nn.gelu(x, approximate=True)

def _silu(x):
    return jax.nn.silu(x)

def _sigmoid(x):
    return jax.nn.sigmoid(x)

def _layernorm(x, axis=-1, eps=1e-05):
    m = jnp.mean(x, axis=axis, keepdims=True)
    v = jnp.var(x, axis=axis, keepdims=True)
    return (x - m) / jnp.sqrt(v + eps)

def _scatter_add(tgt, idx, src, axis=0):
    return tgt.at[idx].add(src)

def _segment_sum(src, seg, n):
    return jax.ops.segment_sum(src, seg, n)
kernel_name = 'mk_adj_resnorm_d2_adj_r2_86e014'

def setup_inputs(seed: int=0):
    np.random.seed(seed)
    _w = jnp.asarray

    def _rec_inputs():
        import jax
        import jax.numpy as jnp
        _gk = jax.random.key(seed)
        x = -0.0002928 + 1 * jax.random.normal(jax.random.fold_in(_gk, 1), (16, 512, 256), jnp.float32)
        _a = jax.random.bernoulli(jax.random.fold_in(_gk, 2), 0.00390625, (16, 512, 512))
        _a = jnp.logical_or(_a, jnp.swapaxes(_a, -1, -2))
        _a = jnp.logical_or(_a, jnp.eye(512, dtype=bool))
        adj = _a.astype(jnp.int32)
        return (x, adj)
    x, adj = _rec_inputs()

    def _L0_gnn_setup():
        import jax, jax.numpy as jnp
        import numpy as np
        L = 3
        D = 256
        B, N = (8, 512)
        EPS = 1e-05

        def layernorm(x, gamma, beta):
            mu = jnp.mean(x, axis=-1, keepdims=True)
            var = jnp.var(x, axis=-1, keepdims=True)
            return (x - mu) * jax.lax.rsqrt(var + EPS) * gamma + beta
        key = jax.random.key(seed)
        ks = jax.random.split(key, 12)
        s = 1.0 / np.sqrt(D)
        node_features = jax.random.normal(ks[0], (B, N, D), dtype=jnp.float32)
        adjacency_matrix = jax.random.randint(ks[1], (B, N, N), 0, 2, dtype=jnp.int32)
        return {'node_features': node_features, 'adjacency_matrix': adjacency_matrix, 'attn_w': jax.random.normal(ks[2], (L, 2 * D), dtype=jnp.float32) * (1.0 / np.sqrt(2 * D)), 'attn_b': jax.random.normal(ks[3], (L,), dtype=jnp.float32) * 0.01, 'W1': jax.random.normal(ks[4], (L, D, 4 * D), dtype=jnp.float32) * s, 'b1': jnp.zeros((L, 4 * D), dtype=jnp.float32), 'W2': jax.random.normal(ks[5], (L, 4 * D, D), dtype=jnp.float32) * (1.0 / np.sqrt(4 * D)), 'b2': jnp.zeros((L, D), dtype=jnp.float32), 'g1': jnp.ones((L, D), dtype=jnp.float32), 'beta1': jnp.zeros((L, D), dtype=jnp.float32), 'g2': jnp.ones((L, D), dtype=jnp.float32), 'beta2': jnp.zeros((L, D), dtype=jnp.float32)}
    _L0_gnn_all = _L0_gnn_setup()
    _L0_gnn_in = {k: v for k, v in _L0_gnn_all.items() if k in ('attn_w', 'attn_b', 'W1', 'b1', 'W2', 'b2', 'g1', 'beta1', 'g2', 'beta2')}
    del _L0_gnn_all

    def _L1_gnn_setup():
        import jax, jax.numpy as jnp
        import numpy as np
        ALPHA = 0.2
        K_NUM = 16
        NEG_INF = -9000000000000000.0
        key = jax.random.key(seed)
        k1, k2, k3, k4 = jax.random.split(key, 4)
        B, N, F_in, F_out = (4, 1024, 256, 256)
        h = jax.random.normal(k1, (B, N, F_in), dtype=jnp.float32)
        adj = jax.random.randint(k2, (B, N, N), 0, 2, dtype=jnp.int32)

        def xavier(k, shape, gain=1.414):
            fan_in, fan_out = (shape[0], shape[1])
            bound = gain * np.sqrt(6.0 / (fan_in + fan_out))
            return jax.random.uniform(k, shape, jnp.float32, -bound, bound)
        W = xavier(k3, (F_in, F_out))
        a = xavier(k4, (2 * F_out, 1))
        return {'h': h, 'adj': adj, 'W': W, 'a': a}
    _L1_gnn_all = _L1_gnn_setup()
    _L1_gnn_in = {k: v for k, v in _L1_gnn_all.items() if k in ('W', 'a')}
    del _L1_gnn_all
    return {'x': x, 'adj': adj, 'L0_gnn_attn_w': _L0_gnn_in['attn_w'], 'L0_gnn_attn_b': _L0_gnn_in['attn_b'], 'L0_gnn_W1': _L0_gnn_in['W1'], 'L0_gnn_b1': _L0_gnn_in['b1'], 'L0_gnn_W2': _L0_gnn_in['W2'], 'L0_gnn_b2': _L0_gnn_in['b2'], 'L0_gnn_g1': _L0_gnn_in['g1'], 'L0_gnn_beta1': _L0_gnn_in['beta1'], 'L0_gnn_g2': _L0_gnn_in['g2'], 'L0_gnn_beta2': _L0_gnn_in['beta2'], 'L1_gnn_W': _L1_gnn_in['W'], 'L1_gnn_a': _L1_gnn_in['a']}

def reference(x, adj, L0_gnn_attn_w, L0_gnn_attn_b, L0_gnn_W1, L0_gnn_b1, L0_gnn_W2, L0_gnn_b2, L0_gnn_g1, L0_gnn_beta1, L0_gnn_g2, L0_gnn_beta2, L1_gnn_W, L1_gnn_a):
    import jax
    import jax.numpy as jnp

    def _L0_gnn_ref(node_features, adjacency_matrix, attn_w, attn_b, W1, b1, W2, b2, g1, beta1, g2, beta2):
        import jax, jax.numpy as jnp
        import numpy as np
        L = 3
        D = 256
        B, N = (8, 512)
        EPS = 1e-05

        def layernorm(x, gamma, beta):
            mu = jnp.mean(x, axis=-1, keepdims=True)
            var = jnp.var(x, axis=-1, keepdims=True)
            return (x - mu) * jax.lax.rsqrt(var + EPS) * gamma + beta
        n = adjacency_matrix.shape[-1]
        mask = adjacency_matrix.astype(jnp.float32) + jnp.eye(n, dtype=jnp.float32) > 0
        x = node_features
        d = x.shape[-1]
        for l in range(attn_w.shape[0]):
            si = x @ attn_w[l, :d]
            sj = x @ attn_w[l, d:]
            scores = si[:, :, None] + sj[:, None, :] + attn_b[l]
            scores = jnp.where(scores >= 0, scores, 0.2 * scores)
            scores = jnp.where(mask, scores, -jnp.inf)
            attn = jax.nn.softmax(scores, axis=-1)
            agg = jnp.einsum('bij,bjd->bid', attn, x)
            h = layernorm(x + agg, g1[l], beta1[l])
            ff = jax.nn.gelu(h @ W1[l] + b1[l], approximate=False) @ W2[l] + b2[l]
            x = layernorm(h + ff, g2[l], beta2[l])
        return x

    def _L1_gnn_ref(h, adj, W, a):
        import jax, jax.numpy as jnp
        import numpy as np
        ALPHA = 0.2
        K_NUM = 16
        NEG_INF = -9000000000000000.0
        F_out = W.shape[1]
        Wh = jnp.einsum('bnf,fo->bno', h, W)
        a1, a2 = (a[:F_out, 0], a[F_out:, 0])
        e_src = Wh @ a1
        e_dst = Wh @ a2
        e = e_src[:, :, None] + e_dst[:, None, :]
        e = jnp.where(e > 0, e, ALPHA * e)
        e = jnp.where(adj > 0, e, NEG_INF)
        attention = jax.nn.softmax(e, axis=2)
        topk_vals = jax.lax.top_k(attention, K_NUM)[0]
        kth = topk_vals[:, :, -1:]
        attention = jnp.where(attention < kth, 0.0, attention)
        h_prime = jnp.einsum('bij,bjo->bio', attention, Wh)
        return jax.nn.elu(h_prime)
    x = _layernorm(x + _L0_gnn_ref(x, adj, L0_gnn_attn_w, L0_gnn_attn_b, L0_gnn_W1, L0_gnn_b1, L0_gnn_W2, L0_gnn_b2, L0_gnn_g1, L0_gnn_beta1, L0_gnn_g2, L0_gnn_beta2), axis=-1)
    x = _layernorm(x + _L1_gnn_ref(x, adj, L1_gnn_W, L1_gnn_a), axis=-1)
    return x

_drawn_inputs = setup_inputs


def setup_inputs(seed=0):
    import zlib

    import numpy as np

    out = dict(_drawn_inputs(seed))
    spreads = {'L0_gnn_b1': (0.0, 0.1),
     'L0_gnn_b2': (0.0, 0.1),
     'L0_gnn_g1': (1.0, 0.2),
     'L0_gnn_beta1': (0.0, 0.1),
     'L0_gnn_g2': (1.0, 0.2),
     'L0_gnn_beta2': (0.0, 0.1)}
    factors = {'L0_gnn_attn_b': 64.0}
    for name, (base, spread) in spreads.items():
        noise = np.random.default_rng([zlib.crc32(name.encode()), seed]).standard_normal(out[name].shape)
        drawn = base * np.exp(spread * noise) if base else spread * noise
        out[name] = jnp.asarray(drawn.astype(out[name].dtype))
    for name, factor in factors.items():
        out[name] = (out[name] * factor).astype(out[name].dtype)
    return out
```

```python
import concourse.bass as bass
from concourse import mybir
from contextlib import ExitStack


B, N, D, F = 16, 512, 256, 1024
FFN_LAYERS = 3
LAST = FFN_LAYERS
LAYERS = FFN_LAYERS + 1
P = 128
NT = N // P
DT = D // P
FT = F // P
EPS = 1e-5
SLOPE = 0.2
MASKED = 9e15
TOP = 16
STREAMS = LAYERS
ORDER = (2, 1, 0, 3)
ROUNDS = B + LAYERS - 1
SLOTS = ROUNDS * LAYERS
BODY = STREAMS * LAYERS
FIRST_STEP = -3
LOOP_FIRST = (LAYERS - 1) * LAYERS + 1
LOOP_COUNT = (SLOTS - LAYERS * (LAYERS - 1) - 3 - LOOP_FIRST) // BODY


def slot(j):
    if not 0 <= j < SLOTS:
        return None
    layer = ORDER[j % LAYERS]
    b = j // LAYERS - layer
    return (layer, b) if 0 <= b < B else None


def is_ffn(j):
    return slot(j) is not None and slot(j)[0] < FFN_LAYERS


def is_last(j):
    return slot(j) is not None and slot(j)[0] == LAST


def is_skip(j):
    return slot(j) is not None and slot(j)[0] == FFN_LAYERS - 1


def is_first(j):
    return slot(j) is not None and slot(j)[0] == 0


def is_any(j):
    return slot(j) is not None


def is_set_up(j):
    return is_first(j) or is_last(j)


def before(kind, j):
    return sum(1 for m in range(max(0, min(j, SLOTS))) if kind(m))


class Step:

    def __init__(self, k, turn=None):
        self.k, self.turn = k, turn

    def count(self, kind, j, per, extra=0):
        c = per * before(kind, j) + extra
        if self.turn is None:
            return c
        return self.turn * (per * (before(kind, LOOP_FIRST + BODY) - before(kind, LOOP_FIRST))) + c

    def batch(self, j):
        b = slot(j)[1]
        return b if self.turn is None else self.turn * STREAMS + b


def run_steps(engine, step):
    for k in range(FIRST_STEP, LOOP_FIRST):
        step(Step(k))
    with engine.Fori(0, LOOP_COUNT) as turn:
        for k in range(LOOP_FIRST, LOOP_FIRST + BODY):
            step(Step(k, turn))
    for k in range(LOOP_FIRST + LOOP_COUNT * BODY, SLOTS):
        step(Step(k))


def gnn_kernel(nc, x, adj, attn_w, attn_b, W1, b1, W2, b2, g1, beta1, g2, beta2, W, a, out):
    f32, f32r, bf16, i32 = (mybir.dt.float32, mybir.dt.float32r, mybir.dt.bfloat16, mybir.dt.int32)
    ALU = mybir.AluOpType
    ACT = mybir.ActivationFunctionType

    x_v = x.rearrange("b (t p) d -> b p t d", p=P)
    out_v = out.rearrange("b (t p) d -> b p t d", p=P)
    adj_v = adj.rearrange("b (t p) j -> b t p j", p=P)

    ctx = ExitStack()
    with ctx:
        def sb(name, shape, dt=f32):
            return ctx.enter_context(nc.sbuf_tensor(name, shape, dt))

        def bank(name):
            return ctx.enter_context(nc.psum_tensor(name, [P, 512], f32))

        def sem(name):
            return ctx.enter_context(nc.semaphore(name))

        w1h = sb("w1h", [P, FFN_LAYERS, DT, F], f32r)
        w1l = sb("w1l", [P, FFN_LAYERS, DT, F], f32r)
        w2h = sb("w2h", [P, FFN_LAYERS, FT, D], f32r)
        w2l = sb("w2l", [P, FFN_LAYERS, FT, D], f32r)
        wg = sb("wg", [P, DT, D])
        attn_b_w = sb("attn_b_w", [P, FFN_LAYERS, 2, D])
        a_b = sb("a_b", [P, 2, D])
        b2_b = sb("b2_b", [P, FFN_LAYERS, D])
        g1_b = sb("g1_b", [P, FFN_LAYERS, D])
        beta1_b = sb("beta1_b", [P, FFN_LAYERS, D])
        g2_b = sb("g2_b", [P, FFN_LAYERS, D])
        beta2_b = sb("beta2_b", [P, FFN_LAYERS, D])
        attn_bias = sb("attn_bias", [P, FFN_LAYERS])
        b1_col = sb("b1_col", [P, FFN_LAYERS * FT])
        ident = sb("ident", [P, P])
        minus_half = sb("minus_half", [P, NT])
        waited = sb("waited", [P, NT])

        feat = [sb(f"feat{q}", [P, NT, D]) for q in range(STREAMS)]
        mask = [sb(f"mask{q}", [P, NT, N], bf16) for q in range(STREAMS)]
        adj_in = sb("adj_in", [P, N], i32)
        x_again = sb("x_again", [P, NT, D])
        wh = sb("wh", [P, NT, D])
        prob = sb("prob", [P, NT, N])
        small = sb("small", [P, N])
        probT = sb("probT", [P, 2, N])
        hid = [sb(f"hid{i}", [P, NT, D]) for i in range(2)]
        hTh = sb("hTh", [P, DT, N], f32r)
        hTl = sb("hTl", [P, DT, N], f32r)
        gh = sb("gh", [P, 2, N], f32r)
        gl = sb("gl", [P, 2, N], f32r)

        neg_dot = sb("neg_dot", [P, 2, 2, NT])
        neg_src = sb("neg_src", [P, 2, NT])
        low = sb("low", [P, 2, NT])
        den = sb("den", [P, 2, NT])
        rden = sb("rden", [P, NT])
        top = sb("top", [P, TOP])
        stats = {n: sb(f"stats_{n}", [P, NT, 6]) for n in ("att", "ffn", "skip")}
        mom = {n: sb(f"mom_{n}", [P, NT, 2]) for n in ("att", "ffn", "skip")}
        veps = {n: sb(f"veps_{n}", [P, NT]) for n in ("att", "ffn", "skip")}
        rstd = {n: sb(f"rstd_{n}", [P, NT]) for n in ("att", "ffn", "skip")}

        tb = [bank(f"tb{i}") for i in range(3)]
        fb = [bank(f"fb{i}") for i in range(2)]
        yb = [bank(f"yb{i}") for i in range(2)]
        sj = bank("sj")

        consts_loaded = sem("consts_loaded")
        ident_ready = sem("ident_ready")
        weights_in = [sem(f"weights_in{i}") for i in range(2)]
        weights_hi = sem("weights_hi")
        weights_lo = sem("weights_lo")
        x_loaded = sem("x_loaded")
        adj_loaded = sem("adj_loaded")
        again_loaded = sem("again_loaded")
        stored = sem("stored")
        hT_out = sem("hT_out")
        pT_out = sem("pT_out")
        agg_out = sem("agg_out")
        sj_out = sem("sj_out")
        up_out = sem("up_out")
        down_read = sem("down_read")
        xT_out = sem("xT_out")
        wh_out = sem("wh_out")
        hTh_done = sem("hTh_done")
        pT_copied = sem("pT_copied")
        small_done = sem("small_done")
        exp_done = sem("exp_done")
        gelu_done = sem("gelu_done")
        xT_copied = sem("xT_copied")
        wh_copied = sem("wh_copied")
        elu_exp = sem("elu_exp")
        hTl_done = sem("hTl_done")
        gl_done = sem("gl_done")
        dots_done = sem("dots_done")
        lrelu_done = sem("lrelu_done")
        masked_done = sem("masked_done")
        cut_done = sem("cut_done")
        elu_in = sem("elu_in")
        att_resid = sem("att_resid")
        att_var = sem("att_var")
        att_norm = sem("att_norm")
        ffn_resid = sem("ffn_resid")
        ffn_var = sem("ffn_var")
        ffn_norm = sem("ffn_norm")
        skip_resid = sem("skip_resid")
        skip_var = sem("skip_var")
        skip_norm = sem("skip_norm")
        mask_made = sem("mask_made")
        plus_b2 = sem("plus_b2")
        att_rstd = sem("att_rstd")
        ffn_rstd = sem("ffn_rstd")
        skip_rstd = sem("skip_rstd")

        def stream(j):
            return slot(j)[1] % STREAMS

        chunks = []
        for l in range(FFN_LAYERS):
            for d in range(DT):
                chunks.append((W1[l].rearrange("(d p) n -> p d n", p=P)[:, d, :],
                               w1h[:, l, d, :], w1l[:, l, d, :]))
            for h in range(2):
                rows = slice(h * FT // 2, (h + 1) * FT // 2)
                chunks.append((W2[l].rearrange("(f p) n -> p f n", p=P)[:, rows, :],
                               w2h[:, l, rows, :].rearrange("p f n -> p (f n)"),
                               w2l[:, l, rows, :].rearrange("p f n -> p (f n)")))

        def staged(c):
            return hid[c % 2][:, :, :].rearrange("p t d -> p (t d)")

        def load_views():
            yield wg[:, :, :], W.rearrange("(d p) n -> p d n", p=P)
            yield attn_b_w[:, :, :, :].rearrange("p l s d -> p (l s d)"), attn_w.rearrange("l d -> (l d)")
            yield a_b[:, :, :].rearrange("p s d -> p (s d)"), a.rearrange("d o -> (d o)")
            for dst, src in ((b2_b, b2), (g1_b, g1), (beta1_b, beta1), (g2_b, g2), (beta2_b, beta2)):
                yield dst[:, :, :].rearrange("p l d -> p (l d)"), src.rearrange("l d -> (l d)")
            yield attn_bias[:, :], attn_b

        N_CONSTS = 10

        block = ctx.enter_context(nc.Block())

        @block.sync
        def _(sp):
            for n, (dst, src) in enumerate(load_views()):
                if n:
                    src = src.partition_broadcast(P)
                sp.dma_start(dst, src).then_inc(consts_loaded, 16)
            with nc.allow_non_contiguous_dma(reason="one small load of a bias, turned"):
                sp.dma_start(b1_col[:, :], b1.rearrange("l (f p) -> p (l f)", p=P)).then_inc(consts_loaded, 16)
            for c, (src, hi, lo) in enumerate(chunks):
                if c >= 2:
                    sp.wait_ge(weights_lo, c - 1)
                dst = staged(c)
                if len(src.shape) == 3:
                    dst = dst.rearrange("p (f n) -> p f n", n=D)
                sp.dma_start(dst, src).then_inc(weights_in[c % 2], 16)

            def step(s):
                k = s.k
                if is_skip(k):
                    if before(is_skip, k):
                        sp.wait_ge(skip_resid, s.count(is_skip, k, 1))
                    sp.dma_start(x_again[:, :, :], x_v[s.batch(k)]).then_inc(again_loaded, 16)
                j = k + 3
                if is_first(j):
                    if before(is_any, k + 1):
                        sp.wait_ge(att_resid, s.count(is_any, k + 1, 1))
                    sp.dma_start(feat[stream(j)][:, :, :], x_v[s.batch(j)]).then_inc(x_loaded, 16)
                if is_set_up(j):
                    for t in range(NT):
                        if before(is_set_up, j) or t:
                            sp.wait_ge(mask_made, s.count(is_set_up, j, NT, t))
                        src = adj_v[s.batch(j), t]
                        if is_last(j):
                            src = src[:, t * P:(t + 1) * P]
                        sp.dma_start(adj_in[:, 0:src.shape[1]], src).then_inc(adj_loaded, 16)
                if is_last(k + 1):
                    sp.wait_ge(att_norm, s.count(is_any, k + 2, 1))
                    sp.dma_start(out_v[s.batch(k + 1)], hid[(k + 1) % 2][:, :, :]).then_inc(stored, 16)

            run_steps(sp, step)
            sp.wait_ge(stored, 16 * B)

        @block.gpsimd
        def _(pool):
            g = nc.gpsimd
            g.memset(ident[:, :], 0.0).then_inc(ident_ready, 1)
            g.memset(minus_half[:, :], -0.5).then_inc(ident_ready, 1)
            pool.wait_ge(ident_ready, 2)
            g.affine_select(out=ident[:, :], in_=ident[:, :], compare_op=ALU.not_equal, fill=1.0,
                            base=0, pattern=[[-1, P]], channel_multiplier=1).then_inc(ident_ready, 1)
            pool.wait_ge(ident_ready, 3)
            pool.wait_ge(consts_loaded, 16 * N_CONSTS)

            def power(kind):
                return g.tensor_tensor(rstd[kind][:, :], veps[kind][:, :], minus_half[:, :], ALU.pow)

            def step(s):
                k = s.k
                if is_ffn(k):
                    l = slot(k)[0]
                    pool.wait_ge(hT_out, s.count(is_ffn, k + 1, DT))
                    h = hid[k % 2][:, :, :]
                    bias = b2_b[:, l:l + 1, :].to_broadcast([P, NT, D])
                    g.tensor_tensor(h, h, bias, ALU.add).then_inc(plus_b2, 1)
                if is_skip(k - 1):
                    pool.wait_ge(skip_var, s.count(is_skip, k, 1))
                    power("skip").then_inc(skip_rstd, 1)
                if is_any(k + 1):
                    pool.wait_ge(att_var, s.count(is_any, k + 2, 1))
                    power("att").then_inc(att_rstd, 1)
                j = k + 3
                if is_set_up(j):
                    q = stream(j)
                    for t in range(NT):
                        if t == 0 and before(is_any, k + 2):
                            pool.wait_ge(masked_done, s.count(is_any, k + 2, NT))
                        pool.wait_ge(adj_loaded, s.count(is_set_up, j, 16 * NT, 16 * t + 16))
                        g.tensor_tensor(waited[:, :], minus_half[:, :], minus_half[:, :], ALU.mult)
                        pool.drain()
                        diag = mask[q][:, t, t * P:(t + 1) * P]
                        if is_first(j):
                            g.tensor_scalar(mask[q][:, t, :], adj_in[:, :], 0.0, MASKED, ALU.is_le, ALU.mult)
                            pool.drain()
                            g.affine_select(out=diag, in_=diag, compare_op=ALU.not_equal, fill=0.0, base=0,
                                            pattern=[[-1, P]], channel_multiplier=1).then_inc(mask_made, 1)
                        else:
                            g.tensor_scalar(diag, adj_in[:, 0:P], 0.0, MASKED, ALU.is_le, ALU.mult)\
                             .then_inc(mask_made, 1)
                if is_ffn(k):
                    pool.wait_ge(ffn_var, s.count(is_ffn, k + 1, 1))
                    power("ffn").then_inc(ffn_rstd, 1)

            run_steps(pool, step)

        @block.scalar
        def _(act):
            ac = nc.scalar
            for c, (src, hi, lo) in enumerate(chunks):
                act.wait_ge(weights_in[c % 2], 16 * (c // 2 + 1))
                ac.activation(hi, staged(c), ACT.Copy).then_inc(weights_hi, 1)
            act.wait_ge(consts_loaded, 16 * N_CONSTS)

            def step(s):
                k = s.k
                if is_ffn(k):
                    for d in range(DT):
                        act.wait_ge(hT_out, s.count(is_ffn, k, DT, d + 1))
                        ac.activation(hTh[:, d, :], tb[d][:, :], ACT.Copy).then_inc(hTh_done, 1)
                j = k + 1
                if is_any(j):
                    for t in range(NT):
                        if t == 3 and is_any(j + 1):
                            scaled_scores(s, j + 1)
                        act.wait_ge(pT_out, s.count(is_any, j, NT, t + 1))
                        if t >= 2:
                            act.wait_ge(agg_out, s.count(is_any, j, NT, t - 1))
                        ac.activation(probT[:, t % 2, :], tb[(t + 2) % 3][:, :], ACT.Copy).then_inc(pT_copied, 1)
                elif is_any(j + 1):
                    scaled_scores(s, j + 1)
                j = k + 2
                if is_any(j):
                    for t in range(NT):
                        act.wait_ge(masked_done, s.count(is_any, j, NT, t + 1))
                        ac.activation(prob[:, t, :], prob[:, t, :], ACT.Exp, bias=low[:, j % 2, t:t + 1], scale=-1.0,
                                      accum_out=den[:, j % 2, t:t + 1]).then_inc(exp_done, 1)
                if is_last(k + 1):
                    act.wait_ge(elu_in, s.count(is_last, k + 2, 1))
                    ac.activation(wh[:, :, :], wh[:, :, :], ACT.Exp).then_inc(elu_exp, 1)
                if is_ffn(k):
                    l = slot(k)[0]
                    for f in range(FT):
                        act.wait_ge(up_out, s.count(is_ffn, k, FT, f + 1))
                        if f >= 2:
                            act.wait_ge(down_read, s.count(is_ffn, k, FT, f - 1))
                        b = b1_col[:, l * FT + f:l * FT + f + 1]
                        ac.activation(gh[:, f % 2, :], fb[f % 2][:, :], ACT.Gelu, bias=b)
                        ac.activation(fb[f % 2][:, :], fb[f % 2][:, :], ACT.Gelu, bias=b).then_inc(gelu_done, 1)
                j = k + 3
                if is_last(j):
                    for d in range(DT):
                        act.wait_ge(xT_out, s.count(is_last, j, DT, d + 1))
                        ac.activation(probT[:, d, :], tb[d][:, :], ACT.Copy).then_inc(xT_copied, 1)
                    if before(is_last, j):
                        act.wait_ge(att_resid, s.count(is_any, j - 3, 1))
                    for h in range(2):
                        act.wait_ge(wh_out, s.count(is_last, j, 2, h + 1))
                        rows = wh[:, 2 * h:2 * h + 2, :].rearrange("p t d -> p (t d)")
                        ac.activation(rows, fb[h][:, :], ACT.Copy).then_inc(wh_copied, 1)

            def scaled_scores(s, j):
                act.wait_ge(sj_out, s.count(is_any, j + 1, 1))
                if before(is_any, j):
                    act.wait_ge(lrelu_done, s.count(is_any, j, NT))
                if before(is_last, j):
                    act.wait_ge(cut_done, s.count(is_last, j, NT))
                ac.activation(small[:, :], sj[:, :], ACT.Copy, scale=SLOPE).then_inc(small_done, 1)

            run_steps(act, step)

        @block.vector
        def _(dve):
            v = nc.vector
            for c, (src, hi, lo) in enumerate(chunks):
                dve.wait_ge(weights_hi, c + 1)
                v.tensor_tensor(lo, staged(c), hi.bitcast(f32), ALU.subtract).then_inc(weights_lo, 1)
            dve.wait_ge(consts_loaded, 16 * N_CONSTS)

            def variance(kind, rows, done):
                dve.drain()
                for t in range(NT):
                    v.bn_stats(stats[kind][:, t, :], rows[:, t, :])
                dve.drain()
                for t in range(NT):
                    v.bn_aggr(mom[kind][:, t, :], stats[kind][:, t, :])
                dve.drain()
                v.tensor_scalar(veps[kind][:, :], mom[kind][:, :, 1], EPS, None, ALU.add).then_inc(done, 1)

            def normalise(kind, rows, dst, gamma, beta, done):
                mean = mom[kind][:, :, 0]
                if gamma is None:
                    for t in range(NT):
                        last = v.tensor_scalar(dst[:, t, :], rows[:, t, :], mean[:, t:t + 1], rstd[kind][:, t:t + 1],
                                               ALU.subtract, ALU.mult)
                else:
                    for t in range(NT):
                        v.scalar_tensor_tensor(out=rows[:, t, :], in0=rows[:, t, :], scalar=mean[:, t:t + 1],
                                               in1=gamma, op0=ALU.subtract, op1=ALU.mult)
                    dve.drain()
                    for t in range(NT):
                        last = v.scalar_tensor_tensor(out=dst[:, t, :], in0=rows[:, t, :],
                                                      scalar=rstd[kind][:, t:t + 1], in1=beta,
                                                      op0=ALU.mult, op1=ALU.add)
                last.then_inc(done, 1)

            def cut(s, j, t):
                dve.wait_ge(exp_done, s.count(is_any, j, NT, t + 1))
                v.tensor_copy(top[:, 0:1], low[:, j % 2, t:t + 1])
                dve.drain()
                v.max(top[:, 0:8], prob[:, t, :])
                dve.drain()
                v.match_replace(small[:, :], top[:, 0:8], prob[:, t, :], -1.0)
                dve.drain()
                v.max(top[:, 8:16], small[:, :])
                dve.drain()
                v.scalar_tensor_tensor(out=prob[:, t, :], in0=prob[:, t, :], scalar=top[:, TOP - 1:TOP],
                                       in1=prob[:, t, :], op0=ALU.is_ge, op1=ALU.mult).then_inc(cut_done, 1)

            def scores(s, j):
                q = stream(j)
                dve.wait_ge(small_done, s.count(is_any, j + 1, 1))
                dve.wait_ge(mask_made, s.count(is_set_up, j + 1, NT))
                for t in range(NT):
                    if before(is_any, j):
                        dve.wait_ge(pT_out, s.count(is_any, j - 1, NT, (t + 1) * is_any(j - 1)))
                    v.scalar_tensor_tensor(out=prob[:, t, :], in0=sj[:, :], scalar=neg_src[:, j % 2, t:t + 1],
                                           in1=small[:, :], op0=ALU.add, op1=ALU.min).then_inc(lrelu_done, 1)
                dve.drain()
                for t in range(NT):
                    v.tensor_tensor_reduce(out=prob[:, t, :], in0=prob[:, t, :], in1=mask[q][:, t, :], scale=1.0,
                                           scalar=3e38, op0=ALU.add, op1=ALU.min,
                                           accum_out=low[:, j % 2, t:t + 1]).then_inc(masked_done, 1)

            def dots(s, j):
                l = slot(j)[0]
                dve.drain()
                if l == LAST:
                    rows, vecs = wh, [a_b[:, n, :] for n in range(2)]
                    dve.wait_ge(wh_copied, s.count(is_last, j + 1, 2))
                else:
                    rows, vecs = feat[stream(j)], [attn_b_w[:, l, n, :] for n in range(2)]
                    if l == 0:
                        dve.wait_ge(x_loaded, s.count(is_first, j + 1, 16))
                for n in range(2):
                    for t in range(NT):
                        if t % 2 == 0 and n + t:
                            dve.drain()
                        v.tensor_tensor_reduce(out=sj[:, (t % 2) * D:(t % 2 + 1) * D], in0=rows[:, t, :], in1=vecs[n],
                                               scale=-1.0, scalar=0.0, op0=ALU.mult, op1=ALU.add,
                                               accum_out=neg_dot[:, j % 2, n, t:t + 1])
                dve.drain()
                if l == LAST:
                    v.tensor_scalar(neg_src[:, j % 2, :], neg_dot[:, j % 2, 0, :], 1.0 - SLOPE, None, ALU.mult)\
                     .then_inc(dots_done, 1)
                else:
                    v.tensor_scalar(neg_src[:, j % 2, :], neg_dot[:, j % 2, 0, :], attn_bias[:, l:l + 1], 1.0 - SLOPE,
                                    ALU.subtract, ALU.mult).then_inc(dots_done, 1)

            def attended(s, j):
                q, h = stream(j), hid[j % 2]
                dve.drain()
                if is_last(j - 2):
                    dve.wait_ge(stored, s.count(is_last, j - 1, 16))
                dve.wait_ge(exp_done, s.count(is_any, j + 1, NT))
                v.reciprocal(rden[:, :], den[:, j % 2, :])
                dve.drain()
                for t in range(NT):
                    rows = yb[t // 2][:, (t % 2) * D:(t % 2 + 1) * D]
                    if t % 2 == 0:
                        dve.wait_ge(agg_out, s.count(is_any, j, NT, t + 2))
                    if is_last(j):
                        last = v.tensor_scalar(h[:, t, :], rows, rden[:, t:t + 1], None, ALU.mult)
                    else:
                        last = v.scalar_tensor_tensor(out=h[:, t, :], in0=rows, scalar=rden[:, t:t + 1],
                                                      in1=feat[q][:, t, :], op0=ALU.mult, op1=ALU.add)
                if is_last(j):
                    dve.drain()
                    v.tensor_scalar(wh[:, :, :], h[:, :, :], 0.0, None, ALU.min).then_inc(elu_in, 1)
                    dve.wait_ge(elu_exp, s.count(is_last, j + 1, 1))
                    v.scalar_tensor_tensor(out=wh[:, :, :], in0=wh[:, :, :], scalar=-1.0, in1=feat[q][:, :, :],
                                           op0=ALU.add, op1=ALU.add)
                    dve.drain()
                    last = v.scalar_tensor_tensor(out=h[:, :, :], in0=h[:, :, :], scalar=0.0, in1=wh[:, :, :],
                                                  op0=ALU.max, op1=ALU.add)
                last.then_inc(att_resid, 1)
                variance("att", h, att_var)

            def attended_norm(s, j):
                dve.wait_ge(att_rstd, s.count(is_any, j + 1, 1))
                l, h = slot(j)[0], hid[j % 2]
                if l == LAST:
                    normalise("att", h, h, None, None, att_norm)
                else:
                    normalise("att", h, h, g1_b[:, l, :], beta1_b[:, l, :], att_norm)

            def step(s):
                k = s.k
                if is_ffn(k):
                    for d in range(DT):
                        dve.wait_ge(hTh_done, s.count(is_ffn, k, DT, d + 1))
                        v.tensor_tensor(hTl[:, d, :], tb[d][:, :], hTh[:, d, :].bitcast(f32), ALU.subtract)\
                         .then_inc(hTl_done, 1)
                if is_ffn(k - 1):
                    l, q = slot(k - 1)[0], stream(k - 1)
                    dve.wait_ge(ffn_rstd, s.count(is_ffn, k, 1))
                    normalise("ffn", hid[(k - 1) % 2], feat[q], g2_b[:, l, :], beta2_b[:, l, :], ffn_norm)
                if is_skip(k - 1):
                    dve.drain()
                    dve.wait_ge(again_loaded, s.count(is_skip, k, 16))
                    v.tensor_tensor(feat[q][:, :, :], feat[q][:, :, :], x_again[:, :, :], ALU.add)\
                     .then_inc(skip_resid, 1)
                    variance("skip", feat[q], skip_var)
                if is_any(k + 2):
                    dots(s, k + 2)
                    scores(s, k + 2)
                if is_any(k + 1):
                    attended(s, k + 1)
                late = []
                if is_any(k + 1):
                    late.append(lambda: attended_norm(s, k + 1))
                if is_skip(k - 1):
                    def skip_normalise():
                        dve.wait_ge(skip_rstd, s.count(is_skip, k, 1))
                        normalise("skip", feat[q], feat[q], None, None, skip_norm)
                    late.append(skip_normalise)
                if is_last(k + 2):
                    late += [lambda t=t: cut(s, k + 2, t) for t in range(NT)]
                for f in range(FT):
                    if is_ffn(k):
                        dve.wait_ge(gelu_done, s.count(is_ffn, k, FT, f + 1))
                        v.tensor_tensor(gl[:, f % 2, :], fb[f % 2][:, :], gh[:, f % 2, :].bitcast(f32), ALU.subtract)\
                         .then_inc(gl_done, 1)
                    if late:
                        late.pop(0)()
                if is_ffn(k):
                    dve.wait_ge(down_read, s.count(is_ffn, k + 1, FT))
                    dve.wait_ge(plus_b2, s.count(is_ffn, k + 1, 1))
                    h = hid[k % 2]
                    for i in range(2):
                        rows = h[:, 2 * i:2 * i + 2, :].rearrange("p t d -> p (t d)")
                        last = v.tensor_tensor(rows, yb[i][:, :], rows, ALU.add)
                    last.then_inc(ffn_resid, 1)
                    variance("ffn", h, ffn_var)

            run_steps(dve, step)

        @block.tensor
        def _(pe):
            te = nc.tensor
            pe.wait_ge(ident_ready, 3)
            pe.wait_ge(consts_loaded, 16 * N_CONSTS)
            pe.wait_ge(weights_lo, len(chunks))

            def transpose4(dst, tiles):
                for n, tile in enumerate(tiles):
                    last = te.transpose(dst[:, n * P:(n + 1) * P], tile, ident[:, :])
                return last

            def targets(s, j):
                pe.wait_ge(dots_done, s.count(is_any, j + 1, 1))
                transpose4(sj, [neg_dot[:, j % 2, 1, t:t + 1].to_broadcast([P, P]) for t in range(NT)])\
                    .then_inc(sj_out, 1)

            def step(s):
                k = s.k
                if is_ffn(k):
                    pe.wait_ge(att_norm, s.count(is_any, k + 1, 1))
                    pe.wait_ge(pT_copied, s.count(is_any, k + 1, NT))
                    if before(is_last, k + 3):
                        pe.wait_ge(xT_copied, s.count(is_last, k + 3, DT))
                    for d in range(DT):
                        transpose4(tb[d], [hid[k % 2][:, t, d * P:(d + 1) * P] for t in range(NT)]).then_inc(hT_out, 1)
                j = k + 1
                if is_any(j):
                    x_rows = wh if is_last(j) else feat[stream(j)]

                    def turn(t):
                        if is_last(j):
                            pe.wait_ge(cut_done, s.count(is_last, j, NT, t + 1))
                        else:
                            pe.wait_ge(exp_done, s.count(is_any, j, NT, t + 1))
                        if t in (1, 2) and before(is_ffn, k + 1):
                            pe.wait_ge(hTh_done, s.count(is_ffn, k, DT, t if is_ffn(k) else 0))
                            pe.wait_ge(hTl_done, s.count(is_ffn, k, DT, t if is_ffn(k) else 0))
                        if t in (1, 2) and before(is_last, k + 3):
                            pe.wait_ge(xT_copied, s.count(is_last, k + 3, DT))
                        if t != 3 and before(is_any, j):
                            pe.wait_ge(pT_copied, s.count(is_any, j, NT))
                        if t == 3:
                            pe.wait_ge(pT_copied, s.count(is_any, j, NT, 1))
                        transpose4(tb[(t + 2) % 3], [prob[:, t, i * P:(i + 1) * P] for i in range(NT)])\
                            .then_inc(pT_out, 1)

                    def aggregate(t):
                        pe.wait_ge(pT_copied, s.count(is_any, j, NT, t + 1))
                        for i in range(NT):
                            last = te.matmul(yb[t // 2][:, (t % 2) * D:(t % 2 + 1) * D],
                                             probT[:, t % 2, i * P:(i + 1) * P], x_rows[:, i, :],
                                             start=(i == 0), stop=(i == NT - 1))
                        last.then_inc(agg_out, 1)

                    turn(0)
                    turn(1)
                    if before(is_ffn, k):
                        pe.wait_ge(ffn_resid, s.count(is_ffn, k, 1))
                    if before(is_any, j):
                        pe.wait_ge(att_resid, s.count(is_any, j, 1))
                    aggregate(0)
                    turn(2)
                    aggregate(1)
                    if is_any(j + 1):
                        targets(s, j + 1)
                    aggregate(2)
                    turn(3)
                    aggregate(3)
                elif is_any(j + 1):
                    targets(s, j + 1)
                if is_ffn(k):
                    l = slot(k)[0]

                    def up(f):
                        if f < 2 and before(is_last, k + 3):
                            pe.wait_ge(wh_copied, s.count(is_last, k + 3, 2))
                        if f < 2 and before(is_ffn, k):
                            pe.wait_ge(gl_done, s.count(is_ffn, k, FT))
                        if f >= 2:
                            pe.wait_ge(gl_done, s.count(is_ffn, k, FT, f - 1))
                        cols = slice(f * P, (f + 1) * P)
                        terms = [(w1h, hTh), (w1h, hTl), (w1l, hTh)]
                        for n, (w, h) in enumerate(terms):
                            for d in range(DT):
                                if f == 0 and n < 2:
                                    pe.wait_ge((hTh_done, hTl_done)[n], s.count(is_ffn, k, DT, d + 1))
                                last = te.matmul(fb[f % 2][:, :], w[:, l, d, cols], h[:, d, :],
                                                 start=(n == 0 and d == 0), stop=(n == 2 and d == DT - 1))
                        last.then_inc(up_out, 1)

                    def down(f):
                        if f == 0:
                            pe.wait_ge(att_resid, s.count(is_any, k + 2, 1))
                        pe.wait_ge(gl_done, s.count(is_ffn, k, FT, f + 1))
                        for t in range(NT):
                            rows = yb[t // 2][:, (t % 2) * D:(t % 2 + 1) * D]
                            for n, (g, w) in enumerate([(gh, w2h), (gh, w2l), (gl, w2h)]):
                                last = te.matmul(rows, g[:, f % 2, t * P:(t + 1) * P], w[:, l, f, :],
                                                 start=(f == 0 and n == 0 and t % 2 == 0),
                                                 stop=(f == FT - 1 and n == 2), skip_group_check=True)
                        last.then_inc(down_read, 1)

                    up(0)
                    up(1)
                    for f in range(FT):
                        down(f)
                        if f + 2 < FT:
                            up(f + 2)
                j = k + 3
                if is_last(j):
                    q = stream(j)
                    pe.wait_ge(skip_norm, s.count(is_skip, k, 1))
                    if before(is_any, k + 2):
                        pe.wait_ge(pT_copied, s.count(is_any, k + 2, NT))
                    if before(is_ffn, k + 1):
                        pe.wait_ge(hTl_done, s.count(is_ffn, k + 1, DT))
                        pe.wait_ge(gl_done, s.count(is_ffn, k + 1, FT))
                    for d in range(DT):
                        transpose4(tb[d], [feat[q][:, t, d * P:(d + 1) * P] for t in range(NT)]).then_inc(xT_out, 1)
                    for d in range(DT):
                        pe.wait_ge(xT_copied, s.count(is_last, j, DT, d + 1))
                    for t in range(NT):
                        for d in range(DT):
                            last = te.matmul(fb[t // 2][:, (t % 2) * D:(t % 2 + 1) * D],
                                             probT[:, d, t * P:(t + 1) * P], wg[:, d, :],
                                             start=(d == 0), stop=(d == DT - 1))
                        if t % 2:
                            last.then_inc(wh_out, 1)

            run_steps(pe, step)


_INS = ["x", "adj", "L0_gnn_attn_w", "L0_gnn_attn_b", "L0_gnn_W1", "L0_gnn_b1", "L0_gnn_W2", "L0_gnn_b2",
        "L0_gnn_g1", "L0_gnn_beta1", "L0_gnn_g2", "L0_gnn_beta2", "L1_gnn_W", "L1_gnn_a"]
_OUT = (B, N, D)


def kernel(**inputs):
    import numpy as np
    import concourse.bacc as bacc
    from concourse import mybir as mb
    from concourse.bass_utils import run_bass_kernel_spmd

    nc = bacc.Bacc("TRN2", target_bir_lowering=False, num_devices=1)
    arrays, args = {}, []
    for name in _INS:
        v = np.ascontiguousarray(inputs[name])
        arrays[f"in_{name}"] = v
        args.append(nc.dram_tensor(f"in_{name}", v.shape, mb.dt.from_np(v.dtype), kind="ExternalInput").ap())
    args.append(nc.dram_tensor("out_0", _OUT, mb.dt.float32, kind="ExternalOutput").ap())
    gnn_kernel(nc, *args)
    r = run_bass_kernel_spmd(nc, [arrays], core_ids=[0])
    return r.results[0]["out_0"]
```

```python
import concourse.bass as bass
from concourse import mybir
from contextlib import ExitStack


B, N, D, F = 16, 512, 256, 1024
FFN_LAYERS = 3
LAST = FFN_LAYERS
LAYERS = FFN_LAYERS + 1
P = 128
NT = N // P
DT = D // P
FT = F // P
EPS = 1e-5
SLOPE = 0.2
MASKED = 9e15
TOP = 16
STREAMS = LAYERS
ORDER = (2, 1, 0, 3)
ROUNDS = B + LAYERS - 1
SLOTS = ROUNDS * LAYERS
BODY = STREAMS * LAYERS
FIRST_STEP = -3
LOOP_FIRST = (LAYERS - 1) * LAYERS + 1
LOOP_COUNT = (SLOTS - LAYERS * (LAYERS - 1) - 3 - LOOP_FIRST) // BODY


def slot(j):
    if not 0 <= j < SLOTS:
        return None
    layer = ORDER[j % LAYERS]
    b = j // LAYERS - layer
    return (layer, b) if 0 <= b < B else None


def is_ffn(j):
    return slot(j) is not None and slot(j)[0] < FFN_LAYERS


def is_last(j):
    return slot(j) is not None and slot(j)[0] == LAST


def is_skip(j):
    return slot(j) is not None and slot(j)[0] == FFN_LAYERS - 1


def is_first(j):
    return slot(j) is not None and slot(j)[0] == 0


def is_any(j):
    return slot(j) is not None


def before(kind, j):
    return sum(1 for m in range(max(0, min(j, SLOTS))) if kind(m))


class Step:

    def __init__(self, k, turn=None):
        self.k, self.turn = k, turn

    def count(self, kind, j, per, extra=0):
        c = per * before(kind, j) + extra
        if self.turn is None:
            return c
        return self.turn * (per * (before(kind, LOOP_FIRST + BODY) - before(kind, LOOP_FIRST))) + c

    def batch(self, j):
        b = slot(j)[1]
        return b if self.turn is None else self.turn * STREAMS + b


def run_steps(engine, step):
    for k in range(FIRST_STEP, LOOP_FIRST):
        step(Step(k))
    with engine.Fori(0, LOOP_COUNT) as turn:
        for k in range(LOOP_FIRST, LOOP_FIRST + BODY):
            step(Step(k, turn))
    for k in range(LOOP_FIRST + LOOP_COUNT * BODY, SLOTS + 1):
        step(Step(k))


def gnn_kernel(nc, x, adj, attn_w, attn_b, W1, b1, W2, b2, g1, beta1, g2, beta2, W, a, out):
    f32, f32r, bf16, i32 = (mybir.dt.float32, mybir.dt.float32r, mybir.dt.bfloat16, mybir.dt.int32)
    ALU = mybir.AluOpType
    ACT = mybir.ActivationFunctionType

    x_v = x.rearrange("b (t p) d -> b p t d", p=P)
    out_v = out.rearrange("b (t p) d -> b p t d", p=P)
    adj_v = adj.rearrange("b (t p) j -> b p t j", p=P)

    ctx = ExitStack()
    with ctx:
        def sb(name, shape, dt=f32):
            return ctx.enter_context(nc.sbuf_tensor(name, shape, dt))

        def bank(name):
            return ctx.enter_context(nc.psum_tensor(name, [P, 512], f32))

        def sem(name):
            return ctx.enter_context(nc.semaphore(name))

        w1h = sb("w1h", [P, FFN_LAYERS, DT, F], f32r)
        w1l = sb("w1l", [P, FFN_LAYERS, DT, F], f32r)
        w2h = sb("w2h", [P, FFN_LAYERS, FT, D], f32r)
        w2l = sb("w2l", [P, FFN_LAYERS, FT, D], f32r)
        wg = sb("wg", [P, DT, D])
        attn_b_w = sb("attn_b_w", [P, FFN_LAYERS, 2, D])
        a_b = sb("a_b", [P, 2, D])
        b2_b = sb("b2_b", [P, FFN_LAYERS, D])
        g1_b = sb("g1_b", [P, FFN_LAYERS, D])
        beta1_b = sb("beta1_b", [P, FFN_LAYERS, D])
        g2_b = sb("g2_b", [P, FFN_LAYERS, D])
        beta2_b = sb("beta2_b", [P, FFN_LAYERS, D])
        attn_bias = sb("attn_bias", [P, FFN_LAYERS])
        b1_col = sb("b1_col", [P, FFN_LAYERS * FT])
        ident = sb("ident", [P, P])
        minus_half = sb("minus_half", [P, NT])
        waited = sb("waited", [P, NT])

        feat = [sb(f"feat{q}", [P, NT, D]) for q in range(STREAMS)]
        mask = [sb(f"mask{q}", [P, NT, N], bf16) for q in range(STREAMS)]
        x_again = sb("x_again", [P, NT, D])
        wh = sb("wh", [P, NT, D])
        prob = [sb(f"prob{i}", [P, NT, N]) for i in range(2)]
        small = sb("small", [P, N])
        relu = sb("relu", [P, N])
        hid = [sb(f"hid{i}", [P, NT, D]) for i in range(2)]
        hTh = sb("hTh", [P, DT, N], f32r)
        hTl = sb("hTl", [P, DT, N], f32r)
        gh = sb("gh", [P, 2, N], f32r)
        gl = sb("gl", [P, 2, N], f32r)

        dot = sb("dot", [P, 2, 2, NT])
        source = sb("source", [P, 2, NT])
        carrier = sb("carrier", [P, NT])
        low = sb("low", [P, 2, NT])
        den = sb("den", [P, 2, NT])
        rden = sb("rden", [P, NT])
        top = sb("top", [P, 2, TOP])
        stats = {n: sb(f"stats_{n}", [P, NT, 6]) for n in ("att", "fin", "ffn", "skip")}
        mom = {n: sb(f"mom_{n}", [P, NT, 2]) for n in ("att", "fin", "ffn", "skip")}
        veps = {n: sb(f"veps_{n}", [P, NT]) for n in ("att", "fin", "ffn", "skip")}
        rstd = {n: sb(f"rstd_{n}", [P, NT]) for n in ("att", "fin", "ffn", "skip")}

        tb = [bank(f"tb{i}") for i in range(2)]
        fb = [bank(f"fb{i}") for i in range(2)]
        yb = [bank(f"yb{i}") for i in range(2)]
        ab = [bank(f"ab{i}") for i in range(2)]
        sj = tb[0]

        consts_loaded = sem("consts_loaded")
        ident_ready = sem("ident_ready")
        weights_in = [sem(f"weights_in{i}") for i in range(2)]
        weights_hi = sem("weights_hi")
        weights_lo = sem("weights_lo")
        x_loaded = sem("x_loaded")
        adj_loaded = sem("adj_loaded")
        diag_loaded = sem("diag_loaded")
        again_loaded = sem("again_loaded")
        stored = sem("stored")
        hT_out = sem("hT_out")
        pT_out = sem("pT_out")
        agg_out = sem("agg_out")
        sj_out = sem("sj_out")
        up_out = sem("up_out")
        down_out = sem("down_out")
        xT_out = sem("xT_out")
        wh_out = sem("wh_out")
        hTh_done = sem("hTh_done")
        pT_copied = sem("pT_copied")
        small_done = sem("small_done")
        relu_done = sem("relu_done")
        exp_done = sem("exp_done")
        gelu_done = sem("gelu_done")
        xT_copied = sem("xT_copied")
        wh_copied = sem("wh_copied")
        elu_exp = sem("elu_exp")
        hTl_done = sem("hTl_done")
        gl_done = sem("gl_done")
        dots_done = sem("dots_done")
        masked_done = sem("masked_done")
        cut_done = sem("cut_done")
        elu_in = sem("elu_in")
        ab_read = sem("ab_read")
        att_var = sem("att_var")
        att_norm = sem("att_norm")
        fin_sum = sem("fin_sum")
        fin_var = sem("fin_var")
        fin_norm = sem("fin_norm")
        ffn_sum = sem("ffn_sum")
        ffn_var = sem("ffn_var")
        ffn_norm = sem("ffn_norm")
        skip_sum = sem("skip_sum")
        skip_var = sem("skip_var")
        skip_norm = sem("skip_norm")
        mask_made = sem("mask_made")
        diag_made = sem("diag_made")
        bias_made = sem("bias_made")
        plus_b2 = sem("plus_b2")
        att_rstd = sem("att_rstd")
        fin_rstd = sem("fin_rstd")
        ffn_rstd = sem("ffn_rstd")
        skip_rstd = sem("skip_rstd")

        def stream(j):
            return slot(j)[1] % STREAMS

        chunks = []
        for l in range(FFN_LAYERS):
            for d in range(DT):
                chunks.append((W1[l].rearrange("(d p) n -> p d n", p=P)[:, d, :],
                               w1h[:, l, d, :], w1l[:, l, d, :]))
            for h in range(2):
                rows = slice(h * FT // 2, (h + 1) * FT // 2)
                chunks.append((W2[l].rearrange("(f p) n -> p f n", p=P)[:, rows, :],
                               w2h[:, l, rows, :].rearrange("p f n -> p (f n)"),
                               w2l[:, l, rows, :].rearrange("p f n -> p (f n)")))

        def staged(c):
            return hid[c % 2][:, :, :].rearrange("p t d -> p (t d)")

        def load_views():
            yield wg[:, :, :], W.rearrange("(d p) n -> p d n", p=P)
            yield attn_b_w[:, :, :, :].rearrange("p l s d -> p (l s d)"), attn_w.rearrange("l d -> (l d)")
            yield a_b[:, :, :].rearrange("p s d -> p (s d)"), a.rearrange("d o -> (d o)")
            for dst, src in ((b2_b, b2), (g1_b, g1), (beta1_b, beta1), (g2_b, g2), (beta2_b, beta2)):
                yield dst[:, :, :].rearrange("p l d -> p (l d)"), src.rearrange("l d -> (l d)")
            yield attn_bias[:, :], attn_b

        N_CONSTS = 10

        block = ctx.enter_context(nc.Block())

        @block.sync
        def _(sp):
            for n, (dst, src) in enumerate(load_views()):
                if n:
                    src = src.partition_broadcast(P)
                sp.dma_start(dst, src).then_inc(consts_loaded, 16)
            with nc.allow_non_contiguous_dma(reason="one small load of a bias, turned"):
                sp.dma_start(b1_col[:, :], b1.rearrange("l (f p) -> p (l f)", p=P)).then_inc(consts_loaded, 16)
            for c, (src, hi, lo) in enumerate(chunks):
                if c >= 2:
                    sp.wait_ge(weights_lo, c - 1)
                dst = staged(c)
                if len(src.shape) == 3:
                    dst = dst.rearrange("p (f n) -> p f n", n=D)
                sp.dma_start(dst, src).then_inc(weights_in[c % 2], 16)

            def step(s):
                k = s.k
                if is_skip(k):
                    if before(is_skip, k):
                        sp.wait_ge(skip_sum, s.count(is_skip, k, 1))
                    sp.dma_start(x_again[:, :, :], x_v[s.batch(k)]).then_inc(again_loaded, 16)
                j = k + 3
                if is_first(j):
                    if is_last(k):
                        sp.wait_ge(fin_sum, s.count(is_last, k + 1, 1))
                    elif before(is_first, j):
                        sp.wait_ge(dots_done, s.count(is_any, j - 3, 1))
                    sp.dma_start(feat[stream(j)][:, :, :], x_v[s.batch(j)]).then_inc(x_loaded, 16)
                if is_last(k - 1):
                    sp.wait_ge(fin_norm, s.count(is_last, k, 1))
                    sp.dma_start(out_v[s.batch(k - 1)], hid[(k - 1) % 2][:, :, :]).then_inc(stored, 16)

            run_steps(sp, step)
            sp.wait_ge(stored, 16 * B)

        @block.gpsimd
        def _(pool):
            g = nc.gpsimd
            g.memset(ident[:, :], 0.0).then_inc(ident_ready, 1)
            g.memset(minus_half[:, :], -0.5).then_inc(ident_ready, 1)
            pool.wait_ge(ident_ready, 2)
            g.affine_select(out=ident[:, :], in_=ident[:, :], compare_op=ALU.not_equal, fill=1.0,
                            base=0, pattern=[[-1, P]], channel_multiplier=1).then_inc(ident_ready, 1)
            pool.wait_ge(ident_ready, 3)
            pool.wait_ge(consts_loaded, 16 * N_CONSTS)

            def power(kind):
                return g.tensor_tensor(rstd[kind][:, :], veps[kind][:, :], minus_half[:, :], ALU.pow)

            def may_wait():
                g.tensor_tensor(waited[:, :], minus_half[:, :], minus_half[:, :], ALU.mult)
                pool.drain()

            def load_adjacency(s, j):
                if is_first(j):
                    if before(is_any, j - 2):
                        pool.wait_ge(bias_made, s.count(is_any, j - 2, NT))
                        may_wait()
                    g.dma_start(mask[stream(j)][:, :, :], adj_v[s.batch(j)]).then_inc(adj_loaded, 16)
                if is_last(j):
                    pool.wait_ge(bias_made, s.count(is_any, j - 6, NT))
                    may_wait()
                    for t in range(NT):
                        cols = slice(t * P, (t + 1) * P)
                        g.dma_start(mask[stream(j)][:, t, cols], adj_v[s.batch(j)][:, t, cols])\
                         .then_inc(diag_loaded, 16)

            def masks(s, j, t):
                if is_first(j):
                    if t == 0:
                        pool.wait_ge(adj_loaded, s.count(is_first, j + 1, 16))
                        may_wait()
                    tile = mask[stream(j)][:, t, :]
                    g.tensor_scalar(tile, tile, 0.0, -MASKED, ALU.is_le, ALU.mult)
                    pool.drain()
                    diag = mask[stream(j)][:, t, t * P:(t + 1) * P]
                    g.affine_select(out=diag, in_=diag, compare_op=ALU.not_equal, fill=0.0, base=0,
                                    pattern=[[-1, P]], channel_multiplier=1).then_inc(mask_made, 1)
                if is_last(j):
                    if t == 0:
                        pool.wait_ge(diag_loaded, s.count(is_last, j + 1, 16 * NT))
                        may_wait()
                    diag = mask[stream(j)][:, t, t * P:(t + 1) * P]
                    g.tensor_scalar(diag, diag, 0.0, -MASKED, ALU.is_le, ALU.mult).then_inc(diag_made, 1)

            def score_bias(s, j, t):
                if t == 0:
                    pool.wait_ge(small_done, s.count(is_any, j + 1, 1))
                    pool.wait_ge(mask_made, s.count(is_first, j + 1, NT))
                    if before(is_last, j + 1):
                        pool.wait_ge(diag_made, s.count(is_last, j + 1, NT))
                g.tensor_tensor(prob[j % 2][:, t, :], small[:, :], mask[stream(j)][:, t, :], ALU.add)\
                 .then_inc(bias_made, 1)

            def step(s):
                k = s.k
                load_adjacency(s, k + 4)
                if is_ffn(k):
                    l = slot(k)[0]
                    pool.wait_ge(hT_out, s.count(is_ffn, k + 1, DT))
                    h = hid[k % 2][:, :, :]
                    bias = b2_b[:, l:l + 1, :].to_broadcast([P, NT, D])
                    g.tensor_tensor(h, h, bias, ALU.add).then_inc(plus_b2, 1)
                masks(s, k + 3, 0)
                masks(s, k + 3, 1)
                if is_skip(k - 1):
                    pool.wait_ge(skip_var, s.count(is_skip, k, 1))
                    power("skip").then_inc(skip_rstd, 1)
                masks(s, k + 3, 2)
                if is_any(k + 2):
                    score_bias(s, k + 2, 0)
                    score_bias(s, k + 2, 1)
                if is_ffn(k + 1):
                    pool.wait_ge(att_var, s.count(is_ffn, k + 2, 1))
                    power("att").then_inc(att_rstd, 1)
                if is_any(k + 2):
                    score_bias(s, k + 2, 2)
                    score_bias(s, k + 2, 3)
                if is_last(k):
                    pool.wait_ge(fin_var, s.count(is_last, k + 1, 1))
                    power("fin").then_inc(fin_rstd, 1)
                if is_ffn(k):
                    pool.wait_ge(ffn_var, s.count(is_ffn, k + 1, 1))
                    power("ffn").then_inc(ffn_rstd, 1)
                masks(s, k + 3, 3)

            run_steps(pool, step)

        @block.scalar
        def _(act):
            ac = nc.scalar
            for c, (src, hi, lo) in enumerate(chunks):
                act.wait_ge(weights_in[c % 2], 16 * (c // 2 + 1))
                ac.activation(hi, staged(c), ACT.Copy).then_inc(weights_hi, 1)
            act.wait_ge(consts_loaded, 16 * N_CONSTS)

            def exponentials(s, j, t):
                act.wait_ge(masked_done, s.count(is_any, j, NT, t + 1))
                p = prob[j % 2][:, t, :]
                ac.activation(p, p, ACT.Exp, bias=low[:, j % 2, t:t + 1], scale=-1.0,
                              accum_out=den[:, j % 2, t:t + 1]).then_inc(exp_done, 1)

            def copy_pT(s, j, t):
                act.wait_ge(pT_out, s.count(is_any, j, NT, t + 1))
                bank = tb[1] if is_last(j) else tb[t % 2]
                ac.activation(prob[j % 2][:, t, :], bank[:, :], ACT.Copy).then_inc(pT_copied, 1)

            def source_scores(s, j, t):
                if t == 0:
                    act.wait_ge(sj_out, s.count(is_any, j + 1, 1))
                    if before(is_any, j):
                        act.wait_ge(bias_made, s.count(is_any, j, NT))
                    ac.activation(small[:, :], sj[:, :], ACT.Copy, scale=SLOPE).then_inc(small_done, 1)
                if before(is_any, j) or t:
                    act.wait_ge(masked_done, s.count(is_any, j, NT, t))
                ac.activation(relu[:, :], sj[:, :], ACT.Relu, bias=source[:, j % 2, t:t + 1], scale=1.0 - SLOPE)\
                  .then_inc(relu_done, 1)

            def step(s):
                k = s.k
                for t in range(NT):
                    if is_any(k + 1):
                        exponentials(s, k + 1, t)
                    if is_ffn(k) and t in (1, 2):
                        d = t - 1
                        act.wait_ge(hT_out, s.count(is_ffn, k, DT, d + 1))
                        ac.activation(hTh[:, d, :], tb[d][:, :], ACT.Copy).then_inc(hTh_done, 1)
                if is_last(k):
                    act.wait_ge(elu_in, s.count(is_last, k + 1, 1))
                    ac.activation(wh[:, :, :], wh[:, :, :], ACT.Exp).then_inc(elu_exp, 1)
                for f in range(FT):
                    if is_ffn(k):
                        l = slot(k)[0]
                        act.wait_ge(up_out, s.count(is_ffn, k, FT, f + 1))
                        if f >= 2:
                            act.wait_ge(down_out, s.count(is_ffn, k, FT, f - 1))
                        b = b1_col[:, l * FT + f:l * FT + f + 1]
                        ac.activation(gh[:, f % 2, :], fb[f % 2][:, :], ACT.Gelu, bias=b)
                        ac.activation(fb[f % 2][:, :], fb[f % 2][:, :], ACT.Gelu, bias=b).then_inc(gelu_done, 1)
                    if is_last(k + 1):
                        if f == 6:
                            copy_pT(s, k + 1, 0)
                        if f >= 4 and is_any(k + 2):
                            source_scores(s, k + 2, f - 4)
                        if f == 7:
                            for t in range(1, NT):
                                copy_pT(s, k + 1, t)
                    else:
                        if is_any(k + 1) and 2 <= f <= 4:
                            if f == 2:
                                copy_pT(s, k + 1, 0)
                            copy_pT(s, k + 1, f - 1)
                        if f >= 4 and is_any(k + 2):
                            source_scores(s, k + 2, f - 4)
                j = k + 3
                if is_last(j):
                    for d in range(DT):
                        act.wait_ge(xT_out, s.count(is_last, j, DT, d + 1))
                        ac.activation(prob[j % 2][:, d, :], tb[d][:, :], ACT.Copy).then_inc(xT_copied, 1)
                    if before(is_last, j):
                        act.wait_ge(fin_sum, s.count(is_last, j, 1))
                    for h in range(2):
                        act.wait_ge(wh_out, s.count(is_last, j, 2, h + 1))
                        rows = wh[:, 2 * h:2 * h + 2, :].rearrange("p t d -> p (t d)")
                        ac.activation(rows, ab[h][:, :], ACT.Copy).then_inc(wh_copied, 1)

            run_steps(act, step)

        @block.vector
        def _(dve):
            v = nc.vector
            for c, (src, hi, lo) in enumerate(chunks):
                dve.wait_ge(weights_hi, c + 1)
                v.tensor_tensor(lo, staged(c), hi.bitcast(f32), ALU.subtract).then_inc(weights_lo, 1)
            dve.wait_ge(consts_loaded, 16 * N_CONSTS)

            def moments(kind, rows, done):
                dve.drain()
                for t in range(NT):
                    v.bn_aggr(mom[kind][:, t, :], stats[kind][:, t, :])
                dve.drain()
                v.tensor_scalar(veps[kind][:, :], mom[kind][:, :, 1], EPS, None, ALU.add).then_inc(done, 1)

            def variance(kind, rows, done):
                dve.drain()
                for t in range(NT):
                    v.bn_stats(stats[kind][:, t, :], rows[:, t, :])
                moments(kind, rows, done)

            def centre(kind, rows, gamma):
                for t in range(NT):
                    v.scalar_tensor_tensor(out=rows[:, t, :], in0=rows[:, t, :], scalar=mom[kind][:, t, 0:1],
                                           in1=gamma, op0=ALU.subtract, op1=ALU.mult)
                dve.drain()

            def scale(kind, rows, dst, beta, done):
                for t in range(NT):
                    last = v.scalar_tensor_tensor(out=dst[:, t, :], in0=rows[:, t, :], scalar=rstd[kind][:, t:t + 1],
                                                  in1=beta, op0=ALU.mult, op1=ALU.add)
                last.then_inc(done, 1)

            def normalise(kind, rows, done):
                for t in range(NT):
                    last = v.tensor_scalar(rows[:, t, :], rows[:, t, :], mom[kind][:, t, 0:1],
                                           rstd[kind][:, t:t + 1], ALU.subtract, ALU.mult)
                last.then_inc(done, 1)

            def cut(s, j, t):
                p, rest = prob[j % 2][:, t, :], ab[1][:, :]
                dve.wait_ge(exp_done, s.count(is_any, j, NT, t + 1))
                v.tensor_copy(carrier[:, t:t + 1], minus_half[:, t:t + 1])
                v.max(top[:, t % 2, 0:8], p)
                dve.drain()
                v.match_replace(rest, top[:, t % 2, 0:8], p, -1.0)
                dve.drain()
                v.max(top[:, t % 2, 8:16], rest)
                dve.drain()
                v.scalar_tensor_tensor(out=p, in0=p, scalar=top[:, t % 2, TOP - 1:TOP], in1=p,
                                       op0=ALU.is_ge, op1=ALU.mult).then_inc(cut_done, 1)

            def masked_scores(s, j, t):
                dve.wait_ge(relu_done, s.count(is_any, j, NT, t + 1))
                dve.wait_ge(bias_made, s.count(is_any, j, NT, t + 1))
                v.tensor_copy(carrier[:, t:t + 1], minus_half[:, t:t + 1])
                p = prob[j % 2][:, t, :]
                v.tensor_tensor_reduce(out=p, in0=p, in1=relu[:, :], scale=-1.0, scalar=3e38, op0=ALU.add,
                                       op1=ALU.min, accum_out=low[:, j % 2, t:t + 1]).then_inc(masked_done, 1)

            def dots(s, j, n):
                l = slot(j)[0]
                if l == LAST:
                    rows, vec = wh, a_b[:, n, :]
                    dve.wait_ge(wh_copied, s.count(is_last, j + 1, 2))
                else:
                    rows, vec = feat[stream(j)], attn_b_w[:, l, n, :]
                    if l == 0:
                        dve.wait_ge(x_loaded, s.count(is_first, j + 1, 16))
                for t in range(NT):
                    v.tensor_tensor_reduce(out=prob[j % 2][:, 2 * n + t // 2, t % 2 * D:(t % 2 + 1) * D],
                                           in0=rows[:, t, :], in1=vec, scale=1.0, scalar=0.0, op0=ALU.mult,
                                           op1=ALU.add, accum_out=dot[:, j % 2, n, t:t + 1])
                if n == 1:
                    dve.drain()
                    bias = 0.0 if l == LAST else attn_bias[:, l:l + 1]
                    v.tensor_scalar(source[:, j % 2, :], dot[:, j % 2, 0, :], bias, 1.0 - SLOPE,
                                    ALU.add, ALU.mult).then_inc(dots_done, 1)

            def attended(s, j, h):
                q, rows = stream(j), hid[j % 2]
                if h == 0:
                    dve.drain()
                    if is_last(j - 2) or is_last(j) and not is_any(j - 2) and before(is_last, j):
                        dve.wait_ge(stored, s.count(is_last, j, 16))
                    dve.wait_ge(exp_done, s.count(is_any, j + 1, NT))
                    v.reciprocal(rden[:, :], den[:, j % 2, :])
                    dve.drain()
                dve.wait_ge(agg_out, s.count(is_any, j, NT, 2 * h + 2))
                for t in (2 * h, 2 * h + 1):
                    got = ab[h][:, (t % 2) * D:(t % 2 + 1) * D]
                    if is_last(j):
                        last = v.tensor_scalar(rows[:, t, :], got, rden[:, t:t + 1], None, ALU.mult)
                    else:
                        last = v.scalar_tensor_tensor(out=rows[:, t, :], in0=got, scalar=rden[:, t:t + 1],
                                                      in1=feat[q][:, t, :], op0=ALU.mult, op1=ALU.add)
                last.then_inc(ab_read, 1)
                if not is_last(j):
                    dve.drain()
                    for t in (2 * h, 2 * h + 1):
                        v.bn_stats(stats["att"][:, t, :], rows[:, t, :])

            def step(s):
                k = s.k
                if is_ffn(k):
                    for d in range(DT):
                        dve.wait_ge(hTh_done, s.count(is_ffn, k, DT, d + 1))
                        v.tensor_tensor(hTl[:, d, :], tb[d][:, :], hTh[:, d, :].bitcast(f32), ALU.subtract)\
                         .then_inc(hTl_done, 1)
                if is_last(k):
                    attended(s, k, 0)
                    attended(s, k, 1)
                    dve.drain()
                    v.tensor_scalar(wh[:, :, :], hid[k % 2][:, :, :], 0.0, None, ALU.min).then_inc(elu_in, 1)
                if is_ffn(k - 1):
                    l, q, h = slot(k - 1)[0], stream(k - 1), hid[(k - 1) % 2]
                    centre("ffn", h, g2_b[:, l, :])
                    dve.wait_ge(ffn_rstd, s.count(is_ffn, k, 1))
                    scale("ffn", h, feat[q], beta2_b[:, l, :], ffn_norm)
                    dve.drain()
                if is_skip(k - 1):
                    dve.wait_ge(again_loaded, s.count(is_skip, k, 16))
                    v.tensor_tensor(feat[q][:, :, :], feat[q][:, :, :], x_again[:, :, :], ALU.add)\
                     .then_inc(skip_sum, 1)
                    variance("skip", feat[q], skip_var)
                if is_last(k - 1):
                    dve.wait_ge(fin_rstd, s.count(is_last, k, 1))
                    normalise("fin", hid[(k - 1) % 2], fin_norm)
                for f in range(FT):
                    if is_ffn(k):
                        dve.wait_ge(gelu_done, s.count(is_ffn, k, FT, f + 1))
                        v.tensor_tensor(gl[:, f % 2, :], fb[f % 2][:, :], gh[:, f % 2, :].bitcast(f32), ALU.subtract)\
                         .then_inc(gl_done, 1)
                    if f < 2 and is_any(k + 2):
                        dots(s, k + 2, f)
                    if f == 2 and is_skip(k - 1):
                        dve.wait_ge(skip_rstd, s.count(is_skip, k, 1))
                        normalise("skip", feat[q], skip_norm)
                    if is_last(k + 1) and 2 <= f < 6:
                        cut(s, k + 1, f - 2)
                    if is_ffn(k + 1):
                        l1, h1 = slot(k + 1)[0], hid[(k + 1) % 2]
                        if f == 3:
                            attended(s, k + 1, 0)
                        if f == 5:
                            attended(s, k + 1, 1)
                            moments("att", h1, att_var)
                        if f == 6:
                            centre("att", h1, g1_b[:, l1, :])
                        if f == 7:
                            dve.wait_ge(att_rstd, s.count(is_ffn, k + 2, 1))
                            scale("att", h1, h1, beta1_b[:, l1, :], att_norm)
                    if f >= 4 and is_any(k + 2):
                        masked_scores(s, k + 2, f - 4)
                if is_last(k):
                    h = hid[k % 2]
                    dve.wait_ge(elu_exp, s.count(is_last, k + 1, 1))
                    v.scalar_tensor_tensor(out=wh[:, :, :], in0=wh[:, :, :], scalar=-1.0,
                                           in1=feat[stream(k)][:, :, :], op0=ALU.add, op1=ALU.add)
                    dve.drain()
                    v.scalar_tensor_tensor(out=h[:, :, :], in0=h[:, :, :], scalar=0.0, in1=wh[:, :, :],
                                           op0=ALU.max, op1=ALU.add).then_inc(fin_sum, 1)
                    variance("fin", h, fin_var)
                if is_ffn(k):
                    h = hid[k % 2]
                    dve.wait_ge(down_out, s.count(is_ffn, k + 1, FT))
                    dve.wait_ge(plus_b2, s.count(is_ffn, k + 1, 1))
                    for i in range(2):
                        rows = h[:, 2 * i:2 * i + 2, :].rearrange("p t d -> p (t d)")
                        last = v.tensor_tensor(rows, yb[i][:, :], rows, ALU.add)
                    last.then_inc(ffn_sum, 1)
                    variance("ffn", h, ffn_var)

            run_steps(dve, step)

        @block.tensor
        def _(pe):
            te = nc.tensor
            pe.wait_ge(ident_ready, 3)
            pe.wait_ge(consts_loaded, 16 * N_CONSTS)
            pe.wait_ge(weights_lo, len(chunks))

            def transpose4(dst, tiles):
                for n, tile in enumerate(tiles):
                    last = te.transpose(dst[:, n * P:(n + 1) * P], tile, ident[:, :])
                return last

            def targets(s, j):
                pe.wait_ge(dots_done, s.count(is_any, j + 1, 1))
                if is_last(j - 1) and is_ffn(j - 2):
                    pe.wait_ge(hTh_done, s.count(is_ffn, j - 2, DT, 1))
                    pe.wait_ge(hTl_done, s.count(is_ffn, j - 2, DT, 1))
                if is_ffn(j - 1):
                    pe.wait_ge(pT_copied, s.count(is_any, j - 1, NT, 3))
                if before(is_any, j):
                    pe.wait_ge(relu_done, s.count(is_any, j, NT))
                if before(is_last, j + 1):
                    pe.wait_ge(xT_copied, s.count(is_last, j + 1, DT))
                transpose4(sj, [dot[:, j % 2, 1, t:t + 1].to_broadcast([P, P]) for t in range(NT)])\
                    .then_inc(sj_out, 1)

            def turn(s, j, t):
                k = j - 1
                if is_last(j):
                    pe.wait_ge(cut_done, s.count(is_last, j, NT, t + 1))
                else:
                    pe.wait_ge(exp_done, s.count(is_any, j, NT, t + 1))
                b = 1 if is_last(j) else t % 2
                if t == b and not is_last(j):
                    if is_ffn(k):
                        pe.wait_ge(hTh_done, s.count(is_ffn, k, DT, b + 1))
                        pe.wait_ge(hTl_done, s.count(is_ffn, k, DT, b + 1))
                    elif before(is_any, j):
                        pe.wait_ge(relu_done, s.count(is_any, j + 1, NT))
                        pe.wait_ge(pT_copied, s.count(is_any, j, NT))
                elif is_last(j):
                    if t:
                        pe.wait_ge(pT_copied, s.count(is_any, j, NT, t))
                    elif is_ffn(k):
                        pe.wait_ge(hTh_done, s.count(is_ffn, k, DT, b + 1))
                        pe.wait_ge(hTl_done, s.count(is_ffn, k, DT, b + 1))
                else:
                    pe.wait_ge(pT_copied, s.count(is_any, j, NT, t - 1))
                if t < 2 and before(is_last, j + 2):
                    pe.wait_ge(xT_copied, s.count(is_last, j + 2, DT))
                transpose4(tb[b], [prob[j % 2][:, t, i * P:(i + 1) * P] for i in range(NT)]).then_inc(pT_out, 1)

            def aggregate(s, j, t):
                x_rows = wh if is_last(j) else feat[stream(j)]
                if t % 2 == 0:
                    if before(is_any, j):
                        pe.wait_ge(ab_read, s.count(is_any, j, 2))
                    if before(is_last, j + 2):
                        pe.wait_ge(wh_copied, s.count(is_last, j + 2, 2))
                pe.wait_ge(pT_copied, s.count(is_any, j, NT, t + 1))
                for i in range(NT):
                    last = te.matmul(ab[t // 2][:, (t % 2) * D:(t % 2 + 1) * D],
                                     prob[j % 2][:, t, i * P:(i + 1) * P], x_rows[:, i, :],
                                     start=(i == 0), stop=(i == NT - 1))
                last.then_inc(agg_out, 1)

            def up(s, k, f):
                l = slot(k)[0]
                if f >= 2:
                    pe.wait_ge(gl_done, s.count(is_ffn, k, FT, f - 1))
                elif before(is_ffn, k):
                    pe.wait_ge(gl_done, s.count(is_ffn, k, FT))
                cols = slice(f * P, (f + 1) * P)
                for n, (w, h) in enumerate([(w1h, hTh), (w1l, hTh), (w1h, hTl)]):
                    for d in range(DT):
                        if f == 0 and n != 1:
                            pe.wait_ge((hTh_done, None, hTl_done)[n], s.count(is_ffn, k, DT, d + 1))
                        last = te.matmul(fb[f % 2][:, :], w[:, l, d, cols], h[:, d, :],
                                         start=(n == 0 and d == 0), stop=(n == 2 and d == DT - 1))
                last.then_inc(up_out, 1)

            def down(s, k, f):
                l = slot(k)[0]
                if f == 0 and before(is_ffn, k):
                    pe.wait_ge(ffn_sum, s.count(is_ffn, k, 1))
                pe.wait_ge(gl_done, s.count(is_ffn, k, FT, f + 1))
                for t in range(NT):
                    rows = yb[t // 2][:, (t % 2) * D:(t % 2 + 1) * D]
                    for n, (g, w) in enumerate([(gh, w2h), (gh, w2l), (gl, w2h)]):
                        last = te.matmul(rows, g[:, f % 2, t * P:(t + 1) * P], w[:, l, f, :],
                                         start=(f == 0 and n == 0 and t % 2 == 0),
                                         stop=(f == FT - 1 and n == 2), skip_group_check=True)
                last.then_inc(down_out, 1)

            def step(s):
                k = s.k
                if is_ffn(k):
                    pe.wait_ge(att_norm, s.count(is_ffn, k + 1, 1))
                    pe.wait_ge(pT_copied, s.count(is_any, k + 1, NT))
                    if before(is_any, k + 2):
                        pe.wait_ge(relu_done, s.count(is_any, k + 2, NT))
                    if before(is_last, k + 3):
                        pe.wait_ge(xT_copied, s.count(is_last, k + 3, DT))
                    for d in range(DT):
                        transpose4(tb[d], [hid[k % 2][:, t, d * P:(d + 1) * P] for t in range(NT)]).then_inc(hT_out, 1)
                    up(s, k, 0)
                    up(s, k, 1)
                for f in range(FT):
                    if is_ffn(k):
                        down(s, k, f)
                        if f + 2 < FT:
                            up(s, k, f + 2)
                    if is_last(k + 1):
                        if f == 2 and is_any(k + 2):
                            targets(s, k + 2)
                        if f >= 4:
                            turn(s, k + 1, f - 4)
                        if f >= 5:
                            aggregate(s, k + 1, f - 5)
                        if f == 7:
                            aggregate(s, k + 1, 3)
                    else:
                        if is_any(k + 1):
                            if f == 0:
                                turn(s, k + 1, 0)
                                turn(s, k + 1, 1)
                            if f in (1, 2):
                                turn(s, k + 1, f + 1)
                            if 1 <= f <= 4:
                                aggregate(s, k + 1, f - 1)
                        if f == 2 and is_any(k + 2):
                            targets(s, k + 2)
                j = k + 3
                if is_last(j):
                    q = stream(j)
                    pe.wait_ge(skip_norm, s.count(is_skip, k, 1))
                    pe.wait_ge(pT_copied, s.count(is_any, k + 2, NT))
                    pe.wait_ge(relu_done, s.count(is_any, k + 3, NT))
                    pe.wait_ge(ab_read, s.count(is_any, k + 2, 2))
                    for d in range(DT):
                        transpose4(tb[d], [feat[q][:, t, d * P:(d + 1) * P] for t in range(NT)]).then_inc(xT_out, 1)
                    for d in range(DT):
                        pe.wait_ge(xT_copied, s.count(is_last, j, DT, d + 1))
                    for t in range(NT):
                        for d in range(DT):
                            last = te.matmul(ab[t // 2][:, (t % 2) * D:(t % 2 + 1) * D],
                                             prob[j % 2][:, d, t * P:(t + 1) * P], wg[:, d, :],
                                             start=(d == 0), stop=(d == DT - 1))
                        if t % 2:
                            last.then_inc(wh_out, 1)

            run_steps(pe, step)


_INS = ["x", "adj", "L0_gnn_attn_w", "L0_gnn_attn_b", "L0_gnn_W1", "L0_gnn_b1", "L0_gnn_W2", "L0_gnn_b2",
        "L0_gnn_g1", "L0_gnn_beta1", "L0_gnn_g2", "L0_gnn_beta2", "L1_gnn_W", "L1_gnn_a"]
_OUT = (B, N, D)


def kernel(**inputs):
    import numpy as np
    import concourse.bacc as bacc
    from concourse import mybir as mb
    from concourse.bass_utils import run_bass_kernel_spmd

    nc = bacc.Bacc("TRN2", target_bir_lowering=False, num_devices=1)
    arrays, args = {}, []
    for name in _INS:
        v = np.ascontiguousarray(inputs[name])
        arrays[f"in_{name}"] = v
        args.append(nc.dram_tensor(f"in_{name}", v.shape, mb.dt.from_np(v.dtype), kind="ExternalInput").ap())
    args.append(nc.dram_tensor("out_0", _OUT, mb.dt.float32, kind="ExternalOutput").ap())
    gnn_kernel(nc, *args)
    r = run_bass_kernel_spmd(nc, [arrays], core_ids=[0])
    return r.results[0]["out_0"]
```

```python
import concourse.bass as bass
from concourse import mybir
from contextlib import ExitStack


B, N, D, F = 16, 512, 256, 1024
FFN_LAYERS = 3
LAST = FFN_LAYERS
LAYERS = FFN_LAYERS + 1
P = 128
NT = N // P
DT = D // P
FT = F // P
EPS = 1e-5
SLOPE = 0.2
MASKED = 9e15
TOP = 16
STREAMS = LAYERS
ORDER = (2, 1, 0, 3)
ROUNDS = B + LAYERS - 1
SLOTS = ROUNDS * LAYERS
HIDDEN = 3
BODY = STREAMS * LAYERS
FIRST_STEP = -3
LOOP_FIRST = (LAYERS - 1) * LAYERS + 2
LOOP_COUNT = (SLOTS - LAYERS * (LAYERS - 1) - 2 - LOOP_FIRST) // BODY


def slot(j):
    if not 0 <= j < SLOTS:
        return None
    layer = ORDER[j % LAYERS]
    b = j // LAYERS - layer
    return (layer, b) if 0 <= b < B else None


def is_ffn(j):
    return slot(j) is not None and slot(j)[0] < FFN_LAYERS


def is_last(j):
    return slot(j) is not None and slot(j)[0] == LAST


def is_skip(j):
    return slot(j) is not None and slot(j)[0] == FFN_LAYERS - 1


def is_first(j):
    return slot(j) is not None and slot(j)[0] == 0


def is_any(j):
    return slot(j) is not None


def on_pool(j):
    return (is_skip(j) or is_first(j)) and LAYERS * (LAYERS - 1) <= j < SLOTS - LAYERS * (LAYERS - 1) - 2


def skip_on_dve(j):
    return is_skip(j) and not on_pool(j)


def before(kind, j):
    return sum(1 for m in range(max(0, min(j, SLOTS))) if kind(m))


def hidden(k, f):
    return (FT * before(is_ffn, k) + f) % HIDDEN


def dots_at(k):
    return (2, 3) if is_last(k + 1) else (6, 6) if is_last(k) else (3, 6)


def scores_at(k):
    return 4 if is_last(k + 1) else 6


class Step:

    def __init__(self, k, turn=None):
        self.k, self.turn = k, turn

    def count(self, kind, j, per, extra=0):
        c = per * before(kind, j) + extra
        if self.turn is None:
            return c
        return self.turn * (per * (before(kind, LOOP_FIRST + BODY) - before(kind, LOOP_FIRST))) + c

    def batch(self, j):
        b = slot(j)[1]
        return b if self.turn is None else self.turn * STREAMS + b


def run_steps(engine, step):
    for k in range(FIRST_STEP, LOOP_FIRST):
        step(Step(k))
    with engine.Fori(0, LOOP_COUNT) as turn:
        for k in range(LOOP_FIRST, LOOP_FIRST + BODY):
            step(Step(k, turn))
    for k in range(LOOP_FIRST + LOOP_COUNT * BODY, SLOTS + 1):
        step(Step(k))


def gnn_kernel(nc, x, adj, attn_w, attn_b, W1, b1, W2, b2, g1, beta1, g2, beta2, W, a, out):
    f32, f32r, bf16 = mybir.dt.float32, mybir.dt.float32r, mybir.dt.bfloat16
    ALU = mybir.AluOpType
    ACT = mybir.ActivationFunctionType

    x_v = x.rearrange("b (t p) d -> b p t d", p=P)
    out_v = out.rearrange("b (t p) d -> b p t d", p=P)
    adj_v = adj.rearrange("b (t p) j -> b p t j", p=P)

    ctx = ExitStack()
    with ctx:
        def sb(name, shape, dt=f32):
            return ctx.enter_context(nc.sbuf_tensor(name, shape, dt))

        def bank(name):
            return ctx.enter_context(nc.psum_tensor(name, [P, 512], f32))

        def sem(name):
            return ctx.enter_context(nc.semaphore(name))

        w1h = sb("w1h", [P, FFN_LAYERS, DT, F], f32r)
        w1l = sb("w1l", [P, FFN_LAYERS, DT, F], f32r)
        w2h = sb("w2h", [P, FFN_LAYERS, FT, D], f32r)
        w2l = sb("w2l", [P, FFN_LAYERS, FT, D], f32r)
        wg = sb("wg", [P, DT, D])
        attn_b_w = sb("attn_b_w", [P, FFN_LAYERS, 2, D])
        a_b = sb("a_b", [P, 2, D])
        b2_b = sb("b2_b", [P, FFN_LAYERS, D])
        g1_b = sb("g1_b", [P, FFN_LAYERS, D])
        beta1_b = sb("beta1_b", [P, FFN_LAYERS, D])
        g2_b = sb("g2_b", [P, FFN_LAYERS, D])
        beta2_b = sb("beta2_b", [P, FFN_LAYERS, D])
        attn_bias = sb("attn_bias", [P, FFN_LAYERS])
        b1_col = sb("b1_col", [P, FFN_LAYERS * FT])
        ident = sb("ident", [P, P])
        minus_half = sb("minus_half", [P, NT])
        waited = sb("waited", [P, NT])

        feat = [sb(f"feat{q}", [P, NT, D]) for q in range(STREAMS)]
        mask = [sb(f"mask{q}", [P, NT, N], bf16) for q in range(STREAMS)]
        wh = sb("wh", [P, NT, D])
        prob = [sb(f"prob{i}", [P, NT, N]) for i in range(2)]
        small = sb("small", [P, N])
        hid = [sb(f"hid{i}", [P, NT, D]) for i in range(2)]
        hTh = sb("hTh", [P, DT, N], f32r)
        hTl = sb("hTl", [P, DT, N], f32r)
        gf = sb("gf", [P, 2, N])
        gh = sb("gh", [P, HIDDEN, N], f32r)
        gl = sb("gl", [P, 2, N], f32r)

        dot = sb("dot", [P, 2, 2, NT])
        source = sb("source", [P, 2, NT])
        carrier = sb("carrier", [P, 3, NT])
        low = sb("low", [P, 2, NT])
        den = sb("den", [P, 2, NT])
        rden = sb("rden", [P, NT])
        top = sb("top", [P, 2, TOP])
        stats = {n: sb(f"stats_{n}", [P, NT, 6]) for n in ("att", "fin", "ffn", "skip")}
        mom = {n: sb(f"mom_{n}", [P, NT, 2]) for n in ("att", "fin", "ffn", "skip")}
        veps = {n: sb(f"veps_{n}", [P, NT]) for n in ("att", "fin", "ffn", "skip")}
        rstd = {n: sb(f"rstd_{n}", [P, NT]) for n in ("att", "fin", "ffn", "skip")}

        tb = [bank(f"tb{i}") for i in range(2)]
        fb = [bank(f"fb{i}") for i in range(2)]
        yb = [bank(f"yb{i}") for i in range(2)]
        ab = [bank(f"ab{i}") for i in range(2)]
        sj = tb[0]

        consts_loaded = sem("consts_loaded")
        ident_ready = sem("ident_ready")
        weights_in = [sem(f"weights_in{i}") for i in range(2)]
        weights_hi = sem("weights_hi")
        weights_lo = sem("weights_lo")
        x_loaded = sem("x_loaded")
        adj_loaded = sem("adj_loaded")
        diag_loaded = sem("diag_loaded")
        skip_added = sem("skip_added")
        stored = sem("stored")
        hT_out = sem("hT_out")
        pT_out = sem("pT_out")
        agg_out = sem("agg_out")
        last_pT_out = sem("last_pT_out")
        last_agg_out = sem("last_agg_out")
        sj_out = sem("sj_out")
        up_out = sem("up_out")
        down_out = sem("down_out")
        xT_out = sem("xT_out")
        wh_out = sem("wh_out")
        hTh_done = sem("hTh_done")
        pT_copied = sem("pT_copied")
        last_pT_copied = sem("last_pT_copied")
        small_done = sem("small_done")
        relu_done = sem("relu_done")
        exp_done = sem("exp_done")
        gelu_done = sem("gelu_done")
        xT_copied = sem("xT_copied")
        wh_copied = sem("wh_copied")
        elu_exp = sem("elu_exp")
        hTl_done = sem("hTl_done")
        gl_done = sem("gl_done")
        dots_done = sem("dots_done")
        masked_done = sem("masked_done")
        cut_done = sem("cut_done")
        elu_in = sem("elu_in")
        ab_read = sem("ab_read")
        last_ab_read = sem("last_ab_read")
        att_var = sem("att_var")
        att_norm = sem("att_norm")
        fin_sum = sem("fin_sum")
        fin_var = sem("fin_var")
        fin_norm = sem("fin_norm")
        ffn_sum = sem("ffn_sum")
        ffn_var = sem("ffn_var")
        skip_var = sem("skip_var")
        skip_norm = sem("skip_norm")
        mask_made = sem("mask_made")
        diag_made = sem("diag_made")
        score_made = sem("score_made")
        plus_b2 = sem("plus_b2")
        att_rstd = sem("att_rstd")
        fin_rstd = sem("fin_rstd")
        ffn_rstd = sem("ffn_rstd")
        skip_rstd = sem("skip_rstd")
        pool_norm = sem("pool_norm")
        dve_norm = sem("dve_norm")

        def stream(j):
            return slot(j)[1] % STREAMS

        chunks = []
        for l in range(FFN_LAYERS):
            for d in range(DT):
                chunks.append((W1[l].rearrange("(d p) n -> p d n", p=P)[:, d, :],
                               w1h[:, l, d, :], w1l[:, l, d, :]))
            for h in range(2):
                rows = slice(h * FT // 2, (h + 1) * FT // 2)
                chunks.append((W2[l].rearrange("(f p) n -> p f n", p=P)[:, rows, :],
                               w2h[:, l, rows, :].rearrange("p f n -> p (f n)"),
                               w2l[:, l, rows, :].rearrange("p f n -> p (f n)")))

        def staged(c):
            return feat[2 + c % 2][:, :, :].rearrange("p t d -> p (t d)")

        def chunks_at(k):
            return range(2 * k + 4, 2 * k + 8) if k in (0, 2) else ()

        def load_views():
            yield wg[:, :, :], W.rearrange("(d p) n -> p d n", p=P)
            yield attn_b_w[:, :, :, :].rearrange("p l s d -> p (l s d)"), attn_w.rearrange("l d -> (l d)")
            yield a_b[:, :, :].rearrange("p s d -> p (s d)"), a.rearrange("d o -> (d o)")
            for dst, src in ((b2_b, b2), (g1_b, g1), (beta1_b, beta1), (g2_b, g2), (beta2_b, beta2)):
                yield dst[:, :, :].rearrange("p l d -> p (l d)"), src.rearrange("l d -> (l d)")
            yield attn_bias[:, :], attn_b

        N_CONSTS = 10

        block = ctx.enter_context(nc.Block())

        @block.sync
        def _(sp):
            for n, (dst, src) in enumerate(load_views()):
                if n:
                    src = src.partition_broadcast(P)
                sp.dma_start(dst, src).then_inc(consts_loaded, 16)
            with nc.allow_non_contiguous_dma(reason="one small load of a bias, turned"):
                sp.dma_start(b1_col[:, :], b1.rearrange("l (f p) -> p (l f)", p=P)).then_inc(consts_loaded, 16)

            def load_chunk(c):
                src, dst = chunks[c][0], staged(c)
                if c >= 2:
                    sp.wait_ge(weights_lo, c - 1)
                if len(src.shape) == 3:
                    dst = dst.rearrange("p (f n) -> p f n", n=D)
                sp.dma_start(dst, src).then_inc(weights_in[c % 2], 16)

            for c in range(4):
                load_chunk(c)

            def step(s):
                k = s.k
                j = k + 3
                if is_first(j):
                    if is_last(k):
                        sp.wait_ge(fin_sum, s.count(is_last, k + 1, 1))
                    elif before(is_first, j):
                        sp.wait_ge(dots_done, s.count(is_any, j - 3, 1))
                    sp.dma_start(feat[stream(j)][:, :, :], x_v[s.batch(j)]).then_inc(x_loaded, 16)
                if k == FIRST_STEP + 2:
                    for c in range(4, len(chunks)):
                        load_chunk(c)
                if is_last(k - 1):
                    sp.wait_ge(fin_norm, s.count(is_last, k, 1))
                    sp.dma_start(out_v[s.batch(k - 1)], wh[:, :, :]).then_inc(stored, 16)

            run_steps(sp, step)
            sp.wait_ge(stored, 16 * B)

        @block.gpsimd
        def _(pool):
            g = nc.gpsimd
            g.memset(ident[:, :], 0.0).then_inc(ident_ready, 1)
            g.memset(minus_half[:, :], -0.5).then_inc(ident_ready, 1)
            pool.wait_ge(ident_ready, 2)
            g.affine_select(out=ident[:, :], in_=ident[:, :], compare_op=ALU.not_equal, fill=1.0,
                            base=0, pattern=[[-1, P]], channel_multiplier=1).then_inc(ident_ready, 1)
            pool.wait_ge(ident_ready, 3)
            pool.wait_ge(consts_loaded, 16 * N_CONSTS)

            def power(kind):
                return g.tensor_tensor(rstd[kind][:, :], veps[kind][:, :], minus_half[:, :], ALU.pow)

            def may_wait():
                g.tensor_tensor(waited[:, :], minus_half[:, :], minus_half[:, :], ALU.mult)
                pool.drain()

            def load_adjacency(s, j):
                if is_first(j):
                    if before(is_any, j - 2):
                        pool.wait_ge(masked_done, s.count(is_any, j - 2, NT))
                        may_wait()
                    g.dma_start(mask[stream(j)][:, :, :], adj_v[s.batch(j)]).then_inc(adj_loaded, 16)
                if is_last(j):
                    pool.wait_ge(masked_done, s.count(is_any, j - 6, NT))
                    may_wait()
                    for t in range(NT):
                        cols = slice(t * P, (t + 1) * P)
                        g.dma_start(mask[stream(j)][:, t, cols], adj_v[s.batch(j)][:, t, cols])\
                         .then_inc(diag_loaded, 16)

            def normalise(j, t):
                row = feat[stream(j)][:, t, :]
                g.tensor_scalar(row, row, mom["ffn"][:, t, 0:1], rstd["ffn"][:, t:t + 1], ALU.subtract, ALU.mult)

            def finish_norm(j):
                rows = feat[stream(j)][:, :, :]
                gamma, beta = (vec[:, slot(j)[0]:slot(j)[0] + 1, :].to_broadcast([P, NT, D])
                               for vec in (g2_b, beta2_b))
                pool.drain()
                g.tensor_tensor(rows, rows, gamma, ALU.mult)
                pool.drain()
                g.tensor_tensor(rows, rows, beta, ALU.add).then_inc(pool_norm, 1)

            def masks(s, j, t):
                if is_first(j):
                    if t == 0:
                        pool.wait_ge(adj_loaded, s.count(is_first, j + 1, 16))
                        may_wait()
                    tile = mask[stream(j)][:, t, :]
                    g.tensor_scalar(tile, tile, 0.0, -MASKED, ALU.is_le, ALU.mult)
                    pool.drain()
                    diag = mask[stream(j)][:, t, t * P:(t + 1) * P]
                    g.affine_select(out=diag, in_=diag, compare_op=ALU.not_equal, fill=0.0, base=0,
                                    pattern=[[-1, P]], channel_multiplier=1).then_inc(mask_made, 1)
                if is_last(j):
                    if t == 0:
                        pool.wait_ge(diag_loaded, s.count(is_last, j + 1, 16 * NT))
                        may_wait()
                    diag = mask[stream(j)][:, t, t * P:(t + 1) * P]
                    g.tensor_scalar(diag, diag, 0.0, -MASKED, ALU.is_le, ALU.mult).then_inc(diag_made, 1)

            def score_sum(s, j, t):
                pool.wait_ge(relu_done, s.count(is_any, j, NT, t + 1))
                p = prob[j % 2][:, t, :]
                g.tensor_tensor(p, p, small[:, :], ALU.add).then_inc(score_made, 1)

            def step(s):
                k = s.k
                if is_ffn(k):
                    l = slot(k)[0]
                    pool.wait_ge(hT_out, s.count(is_ffn, k + 1, DT))
                    h = hid[k % 2][:, :, :]
                    bias = b2_b[:, l:l + 1, :].to_broadcast([P, NT, D])
                    g.tensor_tensor(h, h, bias, ALU.add).then_inc(plus_b2, 1)
                if is_skip(k - 2):
                    pool.wait_ge(skip_var, s.count(is_skip, k - 1, 1))
                    power("skip").then_inc(skip_rstd, 1)
                if is_ffn(k - 1):
                    pool.wait_ge(ffn_var, s.count(is_ffn, k, 1))
                    power("ffn").then_inc(ffn_rstd, 1)
                if is_first(k + 4):
                    load_adjacency(s, k + 4)
                if on_pool(k - 1):
                    pool.drain()
                    for t in range(NT // 2 if is_last(k) else NT):
                        normalise(k - 1, t)
                    if not is_last(k):
                        finish_norm(k - 1)
                if is_skip(k - 1):
                    if on_pool(k - 1):
                        pool.wait_ge(pool_norm, s.count(on_pool, k, 1))
                    else:
                        pool.wait_ge(dve_norm, s.count(skip_on_dve, k, 1))
                    may_wait()
                    g.dma_start(feat[stream(k - 1)][:, :, :], x_v[s.batch(k - 1)], accum_op=ALU.add)\
                     .then_inc(skip_added, 16)
                if is_first(k + 2):
                    for t in range(NT):
                        masks(s, k + 2, t)
                if is_ffn(k + 1):
                    pool.wait_ge(att_var, s.count(is_ffn, k + 2, 1))
                    power("att").then_inc(att_rstd, 1)
                if is_last(k) and on_pool(k - 1):
                    for t in range(NT // 2, NT):
                        normalise(k - 1, t)
                    finish_norm(k - 1)
                if is_last(k - 1):
                    pool.wait_ge(fin_var, s.count(is_last, k, 1))
                    power("fin").then_inc(fin_rstd, 1)
                if is_last(k + 4):
                    load_adjacency(s, k + 4)
                if is_last(k + 2):
                    for t in range(NT):
                        masks(s, k + 2, t)
                if is_any(k + 2):
                    for t in range(NT):
                        score_sum(s, k + 2, t)

            run_steps(pool, step)

        @block.scalar
        def _(act):
            ac = nc.scalar

            def split_high(c):
                act.wait_ge(weights_in[c % 2], 16 * (c // 2 + 1))
                ac.activation(chunks[c][1], staged(c), ACT.Copy).then_inc(weights_hi, 1)

            for c in range(4):
                split_high(c)
            act.wait_ge(consts_loaded, 16 * N_CONSTS)

            def exponentials(s, j, t):
                act.wait_ge(masked_done, s.count(is_any, j, NT, t + 1))
                p = prob[j % 2][:, t, :]
                ac.activation(p, p, ACT.Exp, bias=low[:, j % 2, t:t + 1], scale=-1.0,
                              accum_out=den[:, j % 2, t:t + 1]).then_inc(exp_done, 1)

            def copy_pT(s, j, t):
                if is_last(j):
                    turned, copied, kind = last_pT_out, last_pT_copied, is_last
                else:
                    turned, copied, kind = pT_out, pT_copied, is_ffn
                act.wait_ge(turned, s.count(kind, j, NT, t + 1))
                ac.activation(prob[j % 2][:, t, :], tb[t % 2][:, :], ACT.Copy).then_inc(copied, 1)

            def softmax(s, j):
                for t in range(NT):
                    exponentials(s, j, t)
                    if t >= 2 and not is_last(j):
                        copy_pT(s, j, t - 2)

            def source_scores(s, j, t):
                if t == 0:
                    act.wait_ge(sj_out, s.count(is_any, j + 1, 1))
                    if before(is_any, j):
                        act.wait_ge(score_made, s.count(is_any, j, NT))
                    ac.activation(small[:, :], sj[:, :], ACT.Copy, scale=SLOPE).then_inc(small_done, 1)
                    act.wait_ge(small_done, s.count(is_any, j + 1, 1))
                    if is_last(j - 2):
                        act.wait_ge(last_agg_out, s.count(is_last, j - 1, NT))
                ac.activation(prob[j % 2][:, t, :], small[:, :], ACT.Relu, bias=source[:, j % 2, t:t + 1],
                              scale=(1.0 - SLOPE) / SLOPE).then_inc(relu_done, 1)

            def step(s):
                k = s.k
                for f in range(FT):
                    if is_ffn(k):
                        l = slot(k)[0]
                        act.wait_ge(up_out, s.count(is_ffn, k, FT, f + 1))
                        if f >= HIDDEN or before(is_ffn, k):
                            act.wait_ge(down_out, s.count(is_ffn, k, FT, f + 1 - HIDDEN))
                        if f >= 2 or before(is_ffn, k):
                            act.wait_ge(gl_done, s.count(is_ffn, k, FT, f - 1))
                        if f == 0 and is_last(k - 1):
                            act.wait_ge(cut_done, s.count(is_last, k, NT))
                        b, i = b1_col[:, l * FT + f:l * FT + f + 1], hidden(k, f)
                        ac.activation(gh[:, i, :], fb[f % 2][:, :], ACT.Gelu, bias=b)
                        ac.activation(gf[:, f % 2, :], fb[f % 2][:, :], ACT.Gelu, bias=b).then_inc(gelu_done, 1)
                    if f == 0 and is_any(k + 1) and not is_last(k):
                        for t in range(NT):
                            source_scores(s, k + 1, t)
                    if f == 1 and is_last(k + 2):
                        for d in range(DT):
                            act.wait_ge(xT_out, s.count(is_last, k + 2, DT, d + 1))
                            ac.activation(prob[k % 2][:, d, :], tb[d][:, :], ACT.Copy).then_inc(xT_copied, 1)
                    if is_last(k - 1) and f == 1:
                        act.wait_ge(elu_in, s.count(is_last, k, 1))
                        ac.activation(wh[:, :, :], wh[:, :, :], ACT.Exp).then_inc(elu_exp, 1)
                    if is_any(k + 1) and f == 1 and not is_last(k):
                        softmax(s, k + 1)
                    j = k + 2
                    if f == 1 and is_last(j):
                        if before(is_last, j):
                            act.wait_ge(stored, s.count(is_last, j, 16))
                        for h in range(2):
                            act.wait_ge(wh_out, s.count(is_last, j, 2, h + 1))
                            rows = wh[:, 2 * h:2 * h + 2, :].rearrange("p t d -> p (t d)")
                            ac.activation(rows, ab[h][:, :], ACT.Copy).then_inc(wh_copied, 1)
                    if is_ffn(k + 1):
                        if f == (1 if is_last(k) else 2):
                            copy_pT(s, k + 1, 2)
                            copy_pT(s, k + 1, 3)
                        if f == 6:
                            for d in range(DT):
                                act.wait_ge(hT_out, s.count(is_ffn, k + 1, DT, d + 1))
                                ac.activation(hTh[:, d, :], tb[d][:, :], ACT.Copy).then_inc(hTh_done, 1)
                    if is_last(k) and f in (2, 3, 4, 6):
                        copy_pT(s, k, min(f - 2, 3))
                    if is_last(k + 1):
                        if is_any(k + 2) and f in (5, 6):
                            source_scores(s, k + 2, 2 * f - 10)
                            source_scores(s, k + 2, 2 * f - 9)
                if is_last(k + 1):
                    if is_any(k + 2):
                        softmax(s, k + 2)

                for c in chunks_at(k):
                    split_high(c)

            run_steps(act, step)

        @block.vector
        def _(dve):
            v = nc.vector

            def split_low(c):
                dve.wait_ge(weights_hi, c + 1)
                v.tensor_tensor(chunks[c][2], staged(c), chunks[c][1].bitcast(f32), ALU.subtract)\
                 .then_inc(weights_lo, 1)

            for c in range(4):
                split_low(c)
            dve.wait_ge(consts_loaded, 16 * N_CONSTS)

            def moments(kind, rows, done):
                dve.drain()
                for t in range(NT):
                    v.bn_aggr(mom[kind][:, t, :], stats[kind][:, t, :])
                dve.drain()
                v.tensor_scalar(veps[kind][:, :], mom[kind][:, :, 1], EPS, None, ALU.add).then_inc(done, 1)

            def variance(kind, rows, done):
                dve.drain()
                for t in range(NT):
                    v.bn_stats(stats[kind][:, t, :], rows[:, t, :])
                moments(kind, rows, done)

            def centre(kind, rows, gamma):
                for t in range(NT):
                    v.scalar_tensor_tensor(out=rows[:, t, :], in0=rows[:, t, :], scalar=mom[kind][:, t, 0:1],
                                           in1=gamma, op0=ALU.subtract, op1=ALU.mult)
                dve.drain()

            def scale(kind, rows, beta):
                for t in range(NT):
                    last = v.scalar_tensor_tensor(out=rows[:, t, :], in0=rows[:, t, :], scalar=rstd[kind][:, t:t + 1],
                                                  in1=beta, op0=ALU.mult, op1=ALU.add)
                return last

            def normalise(kind, rows, dst, done):
                for t in range(NT):
                    last = v.tensor_scalar(dst[:, t, :], rows[:, t, :], mom[kind][:, t, 0:1],
                                           rstd[kind][:, t:t + 1], ALU.subtract, ALU.mult)
                last.then_inc(done, 1)

            def cut(s, j, t):
                p, rest = prob[j % 2][:, t, :], ab[1][:, :] if t < 3 else gf[:, 0, :]
                dve.wait_ge(exp_done, s.count(is_any, j, NT, t + 1))
                v.tensor_copy(carrier[:, 0, t:t + 1], minus_half[:, t:t + 1])
                v.max(top[:, t % 2, 0:8], p)
                dve.drain()
                v.match_replace(rest, top[:, t % 2, 0:8], p, -1.0)
                dve.drain()
                v.max(top[:, t % 2, 8:16], rest)
                dve.drain()
                v.scalar_tensor_tensor(out=p, in0=p, scalar=top[:, t % 2, TOP - 1:TOP], in1=p,
                                       op0=ALU.is_ge, op1=ALU.mult).then_inc(cut_done, 1)

            def masked_scores(s, j, t):
                dve.wait_ge(score_made, s.count(is_any, j, NT, t + 1))
                if t == 0:
                    dve.wait_ge(mask_made, s.count(is_first, j + 1, NT))
                    if before(is_last, j + 1):
                        dve.wait_ge(diag_made, s.count(is_last, j + 1, NT))
                v.tensor_copy(carrier[:, 1, t:t + 1], minus_half[:, t:t + 1])
                p = prob[j % 2][:, t, :]
                v.tensor_tensor_reduce(out=p, in0=p, in1=mask[stream(j)][:, t, :], scale=-1.0, scalar=3e38, op0=ALU.add,
                                       op1=ALU.min, accum_out=low[:, j % 2, t:t + 1]).then_inc(masked_done, 1)

            def dots(s, j, n):
                l = slot(j)[0]
                if l == LAST:
                    rows, vec = wh, a_b[:, n, :]
                    dve.wait_ge(wh_copied, s.count(is_last, j + 1, 2))
                else:
                    rows, vec = feat[stream(j)], attn_b_w[:, l, n, :]
                    if on_pool(j - 3) and l == 1:
                        dve.wait_ge(pool_norm, s.count(on_pool, j - 2, 1))
                    if l == 0:
                        dve.wait_ge(x_loaded, s.count(is_first, j + 1, 16))
                for t in range(NT):
                    if is_last(j - 2):
                        products = hid[j % 2][:, t, :]
                    else:
                        products = prob[j % 2][:, 2 * n + t // 2, t % 2 * D:(t % 2 + 1) * D]
                    v.tensor_tensor_reduce(out=products, in0=rows[:, t, :], in1=vec, scale=1.0, scalar=0.0, op0=ALU.mult,
                                           op1=ALU.add, accum_out=dot[:, j % 2, n, t:t + 1])
                if n == 1 or is_last(j - 2):
                    dve.drain()
                if n == 1:
                    bias = 0.0 if l == LAST else attn_bias[:, l:l + 1]
                    v.tensor_scalar(source[:, j % 2, :], dot[:, j % 2, 0, :], bias, 1.0 - SLOPE,
                                    ALU.add, ALU.mult).then_inc(dots_done, 1)

            def attended(s, j, h):
                q, rows = stream(j), hid[j % 2]
                if h == 0:
                    dve.drain()
                    dve.wait_ge(exp_done, s.count(is_any, j + 1, NT))
                    v.reciprocal(rden[:, :], den[:, j % 2, :])
                    dve.drain()
                if is_last(j):
                    dve.wait_ge(last_agg_out, s.count(is_last, j, NT, 2 * h + 2))
                else:
                    dve.wait_ge(agg_out, s.count(is_ffn, j, NT, 2 * h + 2))
                for t in (2 * h, 2 * h + 1):
                    got = ab[h][:, (t % 2) * D:(t % 2 + 1) * D]
                    if is_last(j):
                        last = v.tensor_scalar(rows[:, t, :], got, rden[:, t:t + 1], None, ALU.mult)
                    else:
                        last = v.scalar_tensor_tensor(out=rows[:, t, :], in0=got, scalar=rden[:, t:t + 1],
                                                      in1=feat[q][:, t, :], op0=ALU.mult, op1=ALU.add)
                last.then_inc(last_ab_read if is_last(j) else ab_read, 1)
                if not is_last(j):
                    dve.drain()
                    for t in (2 * h, 2 * h + 1):
                        v.bn_stats(stats["att"][:, t, :], rows[:, t, :])

            def step(s):
                k = s.k
                for f in range(FT):
                    if is_ffn(k):
                        dve.wait_ge(gelu_done, s.count(is_ffn, k, FT, f + 1))
                        if f >= 2 or before(is_ffn, k):
                            dve.wait_ge(down_out, s.count(is_ffn, k, FT, f - 1))
                        high = gh[:, hidden(k, f), :].bitcast(f32)
                        v.tensor_tensor(gl[:, f % 2, :], gf[:, f % 2, :], high, ALU.subtract)\
                         .then_inc(gl_done, 1)
                    if is_any(k + 1) and f == 1 and not is_last(k):
                        for t in range(1, NT):
                            masked_scores(s, k + 1, t)
                    if f == 0:
                        if is_ffn(k - 1):
                            h, x_new = hid[(k - 1) % 2], feat[stream(k - 1)]
                            dve.wait_ge(down_out, s.count(is_ffn, k, FT))
                            dve.wait_ge(plus_b2, s.count(is_ffn, k, 1))
                            for i in range(2):
                                rows, dst = (part[:, 2 * i:2 * i + 2, :].rearrange("p t d -> p (t d)")
                                             for part in (h, x_new))
                                v.tensor_tensor(dst, yb[i][:, :], rows, ALU.add).then_inc(ffn_sum, 1)
                        if is_any(k + 1) and not is_last(k):
                            masked_scores(s, k + 1, 0)
                    if f == 1:
                        if is_ffn(k - 1):
                            variance("ffn", feat[stream(k - 1)], ffn_var)
                    if f == 2 and is_ffn(k - 1) and not on_pool(k - 1):
                        l, rows = slot(k - 1)[0], feat[stream(k - 1)]
                        centre("ffn", rows, g2_b[:, l, :])
                        dve.wait_ge(ffn_rstd, s.count(is_ffn, k, 1))
                        done = scale("ffn", rows, beta2_b[:, l, :])
                        if is_skip(k - 1):
                            done.then_inc(dve_norm, 1)
                        dve.drain()
                    if f == 2 and is_last(k) and is_ffn(k + 1):
                        attended(s, k + 1, 0)
                    if f == 3 and is_last(k) and is_ffn(k + 1):
                        h = hid[(k + 1) % 2]
                        attended(s, k + 1, 1)
                        moments("att", h, att_var)
                        centre("att", h, g1_b[:, slot(k + 1)[0], :])
                    if is_ffn(k + 1):
                        l, h = slot(k + 1)[0], hid[(k + 1) % 2]
                        if f == 3 and not is_last(k):
                            attended(s, k + 1, 0)
                        if f == 4 and not is_last(k):
                            attended(s, k + 1, 1)
                            moments("att", h, att_var)
                            centre("att", h, g1_b[:, l, :])
                        if f == 5:
                            dve.wait_ge(att_rstd, s.count(is_ffn, k + 2, 1))
                            scale("att", h, beta1_b[:, l, :]).then_inc(att_norm, 1)
                    if f == 5 and is_last(k):
                        cut(s, k, 3)
                    if is_ffn(k + 1):
                        if f == 6:
                            for d in range(DT):
                                dve.wait_ge(hTh_done, s.count(is_ffn, k + 1, DT, d + 1))
                                v.tensor_tensor(hTl[:, d, :], tb[d][:, :], hTh[:, d, :].bitcast(f32), ALU.subtract)\
                                 .then_inc(hTl_done, 1)
                    for n in range(2):
                        if is_any(k + 2) and f == dots_at(k)[n]:
                            dots(s, k + 2, n)
                    if is_last(k + 1):
                        if f in (4, 5):
                            cut(s, k + 1, f - 4)
                        if f == 7:
                            if is_any(k + 2):
                                for t in range(NT):
                                    masked_scores(s, k + 2, t)
                            cut(s, k + 1, 2)
                    if f == 7 and is_skip(k - 1):
                        q = stream(k - 1)
                        dve.wait_ge(skip_added, s.count(is_skip, k, 16))
                        v.tensor_copy(carrier[:, 2, :], minus_half[:, :])
                        variance("skip", feat[q], skip_var)
                    if f == 6 and is_last(k):
                        attended(s, k, 0)
                        attended(s, k, 1)
                        dve.drain()
                        v.tensor_scalar(wh[:, :, :], hid[k % 2][:, :, :], 0.0, None, ALU.min).then_inc(elu_in, 1)
                    if is_last(k - 1):
                        if f == 2:
                            dve.wait_ge(elu_exp, s.count(is_last, k, 1))
                            v.scalar_tensor_tensor(out=wh[:, :, :], in0=wh[:, :, :], scalar=-1.0,
                                                   in1=feat[stream(k - 1)][:, :, :], op0=ALU.add, op1=ALU.add)
                            dve.drain()
                            v.scalar_tensor_tensor(out=wh[:, :, :], in0=hid[(k - 1) % 2][:, :, :], scalar=0.0,
                                                   in1=wh[:, :, :], op0=ALU.max, op1=ALU.add).then_inc(fin_sum, 1)
                            variance("fin", wh, fin_var)
                        if f == 7:
                            dve.wait_ge(fin_rstd, s.count(is_last, k, 1))
                            normalise("fin", wh, wh, fin_norm)
                    if f == 7 and is_skip(k - 3):
                        q = stream(k - 3)
                        dve.wait_ge(skip_rstd, s.count(is_skip, k - 2, 1))
                        normalise("skip", feat[q], feat[q], skip_norm)

                for c in chunks_at(k):
                    split_low(c)

            run_steps(dve, step)

        @block.tensor
        def _(pe):
            te = nc.tensor
            pe.wait_ge(ident_ready, 3)
            pe.wait_ge(consts_loaded, 16 * N_CONSTS)

            def transpose4(dst, tiles):
                for n, tile in enumerate(tiles):
                    last = te.transpose(dst[:, n * P:(n + 1) * P], tile, ident[:, :])
                return last

            def targets(s, j):
                pe.wait_ge(dots_done, s.count(is_any, j + 1, 1))
                if is_ffn(j - 1):
                    pe.wait_ge(hTh_done, s.count(is_ffn, j - 1, DT, 1))
                    pe.wait_ge(hTl_done, s.count(is_ffn, j - 1, DT, 1))
                transpose4(sj, [dot[:, j % 2, 1, t:t + 1].to_broadcast([P, P]) for t in range(NT)])\
                    .then_inc(sj_out, 1)

            def turn(s, j, t):
                if is_last(j):
                    pe.wait_ge(cut_done, s.count(is_last, j, NT, t + 1))
                    if t >= 2:
                        pe.wait_ge(last_pT_copied, s.count(is_last, j, NT, t - 1))
                else:
                    pe.wait_ge(exp_done, s.count(is_any, j, NT, t + 1))
                    if t >= 2:
                        pe.wait_ge(pT_copied, s.count(is_ffn, j, NT, t - 1))
                transpose4(tb[t % 2], [prob[j % 2][:, t, i * P:(i + 1) * P] for i in range(NT)])\
                    .then_inc(last_pT_out if is_last(j) else pT_out, 1)

            def aggregate(s, j, t):
                if is_last(j):
                    x_rows, done = wh, last_agg_out
                    if t % 2 == 0 and is_ffn(j + 1):
                        pe.wait_ge(ab_read, s.count(is_ffn, j + 1, 2, t // 2 + 1))
                    pe.wait_ge(last_pT_copied, s.count(is_last, j, NT, t + 1))
                else:
                    x_rows, done = feat[stream(j)], agg_out
                    if t % 2 == 0:
                        if before(is_ffn, j):
                            pe.wait_ge(ab_read, s.count(is_ffn, j, 2))
                        if is_last(j - 2):
                            pe.wait_ge(last_ab_read, s.count(is_last, j, 2))
                        if is_last(j - 1) and t == 2:
                            pe.wait_ge(cut_done, s.count(is_last, j - 1, NT, 3))
                        if is_last(j + 1):
                            pe.wait_ge(wh_copied, s.count(is_last, j + 2, 2))
                    pe.wait_ge(pT_copied, s.count(is_ffn, j, NT, t + 1))
                for i in range(NT):
                    last = te.matmul(ab[t // 2][:, (t % 2) * D:(t % 2 + 1) * D],
                                     prob[j % 2][:, t, i * P:(i + 1) * P], x_rows[:, i, :],
                                     start=(i == 0), stop=(i == NT - 1))
                last.then_inc(done, 1)

            def up(s, k, f):
                l, b = slot(k)
                if b == 0 and f == 0 and s.turn is None:
                    pe.wait_ge(weights_lo, 4 * l + 4)
                if f >= 2 or before(is_ffn, k):
                    pe.wait_ge(gelu_done, s.count(is_ffn, k, FT, f - 1))
                cols = slice(f * P, (f + 1) * P)
                for n, (w, h) in enumerate([(w1h, hTh), (w1l, hTh), (w1h, hTl)]):
                    for d in range(DT):
                        if f == 0 and n != 1:
                            pe.wait_ge((hTh_done, None, hTl_done)[n], s.count(is_ffn, k, DT, d + 1))
                        last = te.matmul(fb[f % 2][:, :], w[:, l, d, cols], h[:, d, :],
                                         start=(n == 0 and d == 0), stop=(n == 2 and d == DT - 1))
                last.then_inc(up_out, 1)

            def down(s, k, f):
                l = slot(k)[0]
                pe.wait_ge(gl_done, s.count(is_ffn, k, FT, f + 1))
                for t in range(NT):
                    if f == 0 and t % 2 == 0 and before(is_ffn, k):
                        pe.wait_ge(ffn_sum, s.count(is_ffn, k, 2, t // 2 - 1))
                    rows = yb[t // 2][:, (t % 2) * D:(t % 2 + 1) * D]
                    for n, (g, w) in enumerate([(gh, w2h), (gh, w2l), (gl, w2h)]):
                        i = hidden(k, f) if g is gh else f % 2
                        last = te.matmul(rows, g[:, i, t * P:(t + 1) * P], w[:, l, f, :],
                                         start=(f == 0 and n == 0 and t % 2 == 0),
                                         stop=(f == FT - 1 and n == 2), skip_group_check=True)
                last.then_inc(down_out, 1)

            def turn_features(s, j):
                q = stream(j)
                pe.wait_ge(skip_norm, s.count(is_skip, j - 3, 1))
                pe.wait_ge(small_done, s.count(is_any, j, 1))
                for d in range(DT):
                    transpose4(tb[d], [feat[q][:, t, d * P:(d + 1) * P] for t in range(NT)]).then_inc(xT_out, 1)

            def features(s, j):
                pe.wait_ge(ab_read, s.count(is_ffn, j - 1, 2))
                for t in range(NT):
                    for d in range(DT):
                        last = te.matmul(ab[t // 2][:, (t % 2) * D:(t % 2 + 1) * D],
                                         prob[j % 2][:, d, t * P:(t + 1) * P], wg[:, d, :],
                                         start=(d == 0), stop=(d == DT - 1))
                    if t % 2:
                        last.then_inc(wh_out, 1)

            def step(s):
                k = s.k
                for f in range(FT):
                    if is_ffn(k + 1) and not is_last(k):
                        if f == 2:
                            turn(s, k + 1, 2)
                        if f == 3:
                            aggregate(s, k + 1, 2)
                            aggregate(s, k + 1, 3)
                    if is_ffn(k):
                        if f + 2 < FT:
                            up(s, k, f + 2)
                        down(s, k, f)
                    if f == 0 and is_last(k + 2):
                        turn_features(s, k + 2)
                    if f == 1 and is_last(k + 2):
                        pe.wait_ge(xT_copied, s.count(is_last, k + 3, DT))
                    if is_ffn(k + 1):
                        if f == 1:
                            turn(s, k + 1, 0)
                            turn(s, k + 1, 1)
                    if f == 1 and is_last(k + 2):
                        features(s, k + 2)
                    if is_ffn(k + 1):
                        if is_last(k):
                            if f == 1:
                                turn(s, k + 1, 2)
                                aggregate(s, k + 1, 0)
                                turn(s, k + 1, 3)
                                for t in range(1, NT):
                                    aggregate(s, k + 1, t)
                        else:
                            if f == 2:
                                turn(s, k + 1, 3)
                            if f in (1, 2):
                                aggregate(s, k + 1, f - 1)
                    if is_last(k):
                        if 2 <= f <= 4:
                            turn(s, k, f - 2)
                        if f == 4:
                            aggregate(s, k, 0)
                    if is_ffn(k + 1):
                        if f == 5:
                            if is_last(k):
                                pe.wait_ge(last_pT_copied, s.count(is_last, k, NT, 3))
                            pe.wait_ge(att_norm, s.count(is_ffn, k + 2, 1))
                            h = hid[(k + 1) % 2]
                            for d in range(DT):
                                transpose4(tb[d], [h[:, t, d * P:(d + 1) * P] for t in range(NT)]).then_inc(hT_out, 1)
                    if f == 5 and is_last(k):
                        aggregate(s, k, 1)
                        aggregate(s, k, 2)
                        if is_ffn(k + 1):
                            pe.wait_ge(hTh_done, s.count(is_ffn, k + 2, DT))
                            pe.wait_ge(hTl_done, s.count(is_ffn, k + 2, DT))
                        turn(s, k, 3)
                    if is_ffn(k + 1):
                        if f == 6:
                            up(s, k + 1, 0)
                    if f == 6 and is_last(k):
                        aggregate(s, k, 3)
                    if is_ffn(k + 1):
                        if f == 7:
                            up(s, k + 1, 1)
                    if f == scores_at(k) and is_any(k + 2):
                        targets(s, k + 2)

            run_steps(pe, step)


_INS = ["x", "adj", "L0_gnn_attn_w", "L0_gnn_attn_b", "L0_gnn_W1", "L0_gnn_b1", "L0_gnn_W2", "L0_gnn_b2",
        "L0_gnn_g1", "L0_gnn_beta1", "L0_gnn_g2", "L0_gnn_beta2", "L1_gnn_W", "L1_gnn_a"]
_OUT = (B, N, D)


def kernel(**inputs):
    import numpy as np
    import concourse.bacc as bacc
    from concourse import mybir as mb
    from concourse.bass_utils import run_bass_kernel_spmd

    nc = bacc.Bacc("TRN2", target_bir_lowering=False, num_devices=1)
    arrays, args = {}, []
    for name in _INS:
        v = np.ascontiguousarray(inputs[name])
        arrays[f"in_{name}"] = v
        args.append(nc.dram_tensor(f"in_{name}", v.shape, mb.dt.from_np(v.dtype), kind="ExternalInput").ap())
    args.append(nc.dram_tensor("out_0", _OUT, mb.dt.float32, kind="ExternalOutput").ap())
    gnn_kernel(nc, *args)
    r = run_bass_kernel_spmd(nc, [arrays], core_ids=[0])
    return r.results[0]["out_0"]
```
